# Optimizing a Trainium2 kernel written in Bass

```python
import numpy as np
import jax
import jax.numpy as jnp

def _softmax(x, axis=-1):
    return jax.nn.softmax(x, axis=axis)

def _gelu(x):
    return jax.nn.gelu(x, approximate=True)

def _silu(x):
    return jax.nn.silu(x)

def _sigmoid(x):
    return jax.nn.sigmoid(x)

def _layernorm(x, axis=-1, eps=1e-05):
    m = jnp.mean(x, axis=axis, keepdims=True)
    v = jnp.var(x, axis=axis, keepdims=True)
    return (x - m) / jnp.sqrt(v + eps)

def _scatter_add(tgt, idx, src, axis=0):
    return tgt.at[idx].add(src)

def _segment_sum(src, seg, n):
    return jax.ops.segment_sum(src, seg, n)
kernel_name = 'mk_decoder_preln_d1_seqx_r8_0a4958'

def setup_inputs(seed: int=0):
    np.random.seed(seed)
    _w = jnp.asarray

    def _rec_inputs():
        import jax
        import jax.numpy as jnp
        _rk = jax.random.key(seed)
        x = 7.22e-05 + 1 * jax.random.normal(jax.random.fold_in(_rk, 1), (8, 56, 128), jnp.float32)
        _lenS = 56 - jax.random.randint(jax.random.fold_in(_rk, 7), (8,), 0, max(1, 56 // 4) + 1, jnp.int32)
        _lenS2 = 1500 - jax.random.randint(jax.random.fold_in(_rk, 8), (8,), 0, max(1, 1500 // 4) + 1, jnp.int32)
        _ctx_1024P = jax.random.normal(jax.random.fold_in(_rk, 11), (8, 16, 128), jnp.float32)
        _ctx_1024c = jax.random.dirichlet(jax.random.fold_in(_rk, 511), 0.3 * jnp.ones((16,), jnp.float32), (8, 1500))
        _ctx_1024t = jnp.einsum('bsk,bkd->bsd', _ctx_1024c, _ctx_1024P)
        _ctx_1024t = _ctx_1024t * jax.lax.rsqrt(jnp.mean(jnp.square(_ctx_1024t)) + 1e-12) * 0.953939
        ctx_1024 = -1.81876e-05 + 0.999925 * (_ctx_1024t + 0.3 * jax.random.normal(jax.random.fold_in(_rk, 611), (8, 1500, 128), jnp.float32))
        _validS = jnp.arange(56)[None, :] < _lenS[:, None]
        _validS2 = jnp.arange(1500)[None, :] < _lenS2[:, None]
        _causal = jnp.tril(jnp.ones((56, 56), dtype=bool))
        mask_BxS2xS_ik0 = jnp.where(jnp.broadcast_to(_validS[:, None, :], (8, 1500, 56)), 0, 1).astype(jnp.int32)
        return (x, ctx_1024, mask_BxS2xS_ik0)
    x, ctx_1024, mask_BxS2xS_ik0 = _rec_inputs()

    def _L0_attn_setup():
        import jax, jax.numpy as jnp
        import numpy as np
        N_EMBD = 128
        BLOCK_SIZE = 256
        B = 8
        LN_EPS = 1e-05

        def _mlp(x, W1, b1, W2, b2):
            h = jax.nn.gelu(x @ W1 + b1, approximate=False)
            return h @ W2 + b2
        key = jax.random.key(seed)
        ks = jax.random.split(key, 14)
        C = N_EMBD
        std = 0.02
        d = {'x': jax.random.normal(ks[0], (B, BLOCK_SIZE, C), dtype=jnp.float32)}
        names = ['q', 'k', 'v']
        i = 1
        for n in names:
            d[f'W1{n}'] = jax.random.normal(ks[i], (C, C), dtype=jnp.float32) * std
            i += 1
            d[f'b1{n}'] = jnp.zeros((C,), dtype=jnp.float32)
            d[f'W2{n}'] = jax.random.normal(ks[i], (C, C), dtype=jnp.float32) * std
            i += 1
            d[f'b2{n}'] = jnp.zeros((C,), dtype=jnp.float32)
        d['ln_w'] = jnp.ones((C,), dtype=jnp.float32)
        d['ln_b'] = jnp.zeros((C,), dtype=jnp.float32)
        return d
    _L0_attn_all = _L0_attn_setup()
    _L0_attn_in = {k: v for k, v in _L0_attn_all.items() if k in ('W1q', 'b1q', 'W2q', 'b2q', 'W1k', 'b1k', 'W2k', 'b2k', 'W1v', 'b1v', 'W2v', 'b2v', 'ln_w', 'ln_b')}
    del _L0_attn_all

    def _L0_xattn_setup():
        import jax, jax.numpy as jnp
        import numpy as np
        B, T, V, C = (32, 32, 125, 128)
        H, DH = (8, 64)
        INNER = H * DH
        K = 5
        SCALE = DH ** (-0.5)

        def layer_norm(x, w, b, eps=1e-05):
            mu = jnp.mean(x, axis=-1, keepdims=True)
            var = jnp.mean(jnp.square(x - mu), axis=-1, keepdims=True)
            return (x - mu) * jax.lax.rsqrt(var + eps) * w + b
        key = jax.random.key(seed)
        ks = jax.random.split(key, 8)
        x = jax.random.normal(ks[0], (B, T, C), dtype=jnp.float32)
        vision = jax.random.normal(ks[1], (B, V, C), dtype=jnp.float32)
        idx = jax.random.randint(ks[2], (B, T, K), 0, V)
        mask = jnp.zeros((B, V, T), jnp.int32)
        mask = mask.at[jnp.arange(B)[:, None, None], idx, jnp.arange(T)[None, :, None]].set(1)
        Wq = jax.random.normal(ks[3], (C, INNER), dtype=jnp.float32) * 0.02
        Wkv = jax.random.normal(ks[4], (C, 2 * INNER), dtype=jnp.float32) * 0.02
        Wout = jax.random.normal(ks[5], (INNER, C), dtype=jnp.float32) * 0.02
        return {'x': x, 'vision': vision, 'ln_w': jnp.ones((C,), jnp.float32), 'ln_b': jnp.zeros((C,), jnp.float32), 'Wq': Wq, 'Wkv': Wkv, 'Wout': Wout, 'attention_mask': mask, 'num_support': K}
    _L0_xattn_all = _L0_xattn_setup()
    _L0_xattn_in = {k: v for k, v in _L0_xattn_all.items() if k in ('ln_w', 'ln_b', 'Wq', 'Wkv', 'Wout')}
    del _L0_xattn_all

    def _L0_ffn_setup():
        import jax, jax.numpy as jnp
        import numpy as np
        TOP_K = 2
        key = jax.random.key(seed)
        ks = jax.random.split(key, 5)
        B, T, D, F, E = (4, 256, 128, 512, 8)
        s = 0.02
        return {'x': jax.random.normal(ks[0], (B, T, D), jnp.float32), 'gate_w': jax.random.normal(ks[1], (D, E), jnp.float32) * s, 'w1': jax.random.normal(ks[2], (E, D, F), jnp.float32) * s, 'w3': jax.random.normal(ks[3], (E, D, F), jnp.float32) * s, 'w2': jax.random.normal(ks[4], (E, F, D), jnp.float32) * s}
    _L0_ffn_all = _L0_ffn_setup()
    _L0_ffn_in = {k: v for k, v in _L0_ffn_all.items() if k in ('gate_w', 'w1', 'w3', 'w2')}
    del _L0_ffn_all
    return {'x': x, 'ctx_1024': ctx_1024, 'mask_BxS2xS_ik0': mask_BxS2xS_ik0, 'L0_attn_W1q': _L0_attn_in['W1q'], 'L0_attn_b1q': _L0_attn_in['b1q'], 'L0_attn_W2q': _L0_attn_in['W2q'], 'L0_attn_b2q': _L0_attn_in['b2q'], 'L0_attn_W1k': _L0_attn_in['W1k'], 'L0_attn_b1k': _L0_attn_in['b1k'], 'L0_attn_W2k': _L0_attn_in['W2k'], 'L0_attn_b2k': _L0_attn_in['b2k'], 'L0_attn_W1v': _L0_attn_in['W1v'], 'L0_attn_b1v': _L0_attn_in['b1v'], 'L0_attn_W2v': _L0_attn_in['W2v'], 'L0_attn_b2v': _L0_attn_in['b2v'], 'L0_attn_ln_w': _L0_attn_in['ln_w'], 'L0_attn_ln_b': _L0_attn_in['ln_b'], 'L0_xattn_ln_w': _L0_xattn_in['ln_w'], 'L0_xattn_ln_b': _L0_xattn_in['ln_b'], 'L0_xattn_Wq': _L0_xattn_in['Wq'], 'L0_xattn_Wkv': _L0_xattn_in['Wkv'], 'L0_xattn_Wout': _L0_xattn_in['Wout'], 'L0_ffn_gate_w': _L0_ffn_in['gate_w'], 'L0_ffn_w1': _L0_ffn_in['w1'], 'L0_ffn_w3': _L0_ffn_in['w3'], 'L0_ffn_w2': _L0_ffn_in['w2']}

def reference(x, ctx_1024, mask_BxS2xS_ik0, L0_attn_W1q, L0_attn_b1q, L0_attn_W2q, L0_attn_b2q, L0_attn_W1k, L0_attn_b1k, L0_attn_W2k, L0_attn_b2k, L0_attn_W1v, L0_attn_b1v, L0_attn_W2v, L0_attn_b2v, L0_attn_ln_w, L0_attn_ln_b, L0_xattn_ln_w, L0_xattn_ln_b, L0_xattn_Wq, L0_xattn_Wkv, L0_xattn_Wout, L0_ffn_gate_w, L0_ffn_w1, L0_ffn_w3, L0_ffn_w2):
    import jax
    import jax.numpy as jnp

    def _L0_attn_ref(x, W1q, b1q, W2q, b2q, W1k, b1k, W2k, b2k, W1v, b1v, W2v, b2v, ln_w, ln_b):
        import jax, jax.numpy as jnp
        import numpy as np
        N_EMBD = 128
        BLOCK_SIZE = 256
        B = 8
        LN_EPS = 1e-05

        def _mlp(x, W1, b1, W2, b2):
            h = jax.nn.gelu(x @ W1 + b1, approximate=False)
            return h @ W2 + b2
        Bsz, T, C = x.shape
        q = _mlp(x, W1q, b1q, W2q, b2q)
        k = _mlp(x, W1k, b1k, W2k, b2k)
        v = _mlp(x, W1v, b1v, W2v, b2v)
        scale = np.sqrt(N_EMBD * BLOCK_SIZE).astype(np.float32)
        scores = jnp.einsum('bid,bjd->bij', q, k) / scale
        mask = jnp.tril(jnp.ones((T, T), dtype=scores.dtype))
        scores = scores * mask
        out = jnp.einsum('bij,bjd->bid', scores, v)
        mu = jnp.mean(out, axis=-1, keepdims=True)
        var = jnp.mean(jnp.square(out - mu), axis=-1, keepdims=True)
        out = (out - mu) * jax.lax.rsqrt(var + LN_EPS) * ln_w + ln_b
        return out

    def _L0_xattn_ref(x, vision, ln_w, ln_b, Wq, Wkv, Wout, attention_mask, num_support):
        import jax, jax.numpy as jnp
        import numpy as np
        B, T, V, C = (32, 32, 125, 128)
        H, DH = (8, 64)
        INNER = H * DH
        K = 5
        SCALE = DH ** (-0.5)

        def layer_norm(x, w, b, eps=1e-05):
            mu = jnp.mean(x, axis=-1, keepdims=True)
            var = jnp.mean(jnp.square(x - mu), axis=-1, keepdims=True)
            return (x - mu) * jax.lax.rsqrt(var + eps) * w + b
        Bb, Tt, Cc = x.shape
        Vv = vision.shape[1]
        am_t = jnp.transpose(attention_mask, (0, 2, 1))
        idxs = jnp.where(am_t != 0, jnp.arange(Vv, dtype=jnp.int32), Vv)
        padded = -jax.lax.top_k(-idxs, num_support)[0]
        vision_pad = jnp.concatenate([vision, jnp.zeros((Bb, 1, Cc), vision.dtype)], axis=1)
        vg = vision_pad[jnp.arange(Bb)[:, None, None], padded]
        valid = padded != Vv
        xn = layer_norm(x, ln_w, ln_b)
        q = jnp.einsum('btc,ce->bte', xn, Wq) * SCALE
        kv = jnp.einsum('btkc,ce->btke', vg, Wkv)
        k, v = jnp.split(kv, 2, axis=-1)
        qh = q.reshape(Bb, Tt, H, DH)
        kh = k.reshape(Bb, Tt, num_support, H, DH)
        vh = v.reshape(Bb, Tt, num_support, H, DH)
        sim = jnp.einsum('bthd,btkhd->bthk', qh, kh)
        sim = sim + jnp.where(valid, 0.0, -10000.0)[:, :, None, :]
        attn = jax.nn.softmax(sim, axis=-1)
        attn = attn * valid[:, :, None, :].astype(attn.dtype)
        out = jnp.einsum('bthk,btkhd->bthd', attn, vh).reshape(Bb, Tt, INNER)
        return jnp.einsum('bte,ec->btc', out, Wout)

    def _L0_ffn_ref(x, gate_w, w1, w3, w2):
        import jax, jax.numpy as jnp
        import numpy as np
        TOP_K = 2
        logits = jnp.einsum('btd,de->bte', x, gate_w)
        probs = jax.nn.softmax(logits, axis=-1)
        expert_weights, expert_indices = jax.lax.top_k(probs, TOP_K)
        expert_weights = expert_weights / expert_weights.sum(-1, keepdims=True)
        E = w1.shape[0]
        out = jnp.zeros_like(x)
        for i in range(E):
            wi = jnp.where(expert_indices == i, expert_weights, 0.0).sum(-1)
            h = jax.nn.silu(jnp.einsum('btd,df->btf', x, w1[i])) * jnp.einsum('btd,df->btf', x, w3[i])
            out = out + jnp.einsum('btf,fd->btd', h, w2[i]) * wi[..., None]
        return out
    x = x + _L0_attn_ref(_layernorm(x, axis=-1), L0_attn_W1q, L0_attn_b1q, L0_attn_W2q, L0_attn_b2q, L0_attn_W1k, L0_attn_b1k, L0_attn_W2k, L0_attn_b2k, L0_attn_W1v, L0_attn_b1v, L0_attn_W2v, L0_attn_b2v, L0_attn_ln_w, L0_attn_ln_b)
    x = x + _L0_xattn_ref(_layernorm(x, axis=-1), ctx_1024, L0_xattn_ln_w, L0_xattn_ln_b, L0_xattn_Wq, L0_xattn_Wkv, L0_xattn_Wout, mask_BxS2xS_ik0, 5)
    x = x + _L0_ffn_ref(_layernorm(x, axis=-1), L0_ffn_gate_w, L0_ffn_w1, L0_ffn_w3, L0_ffn_w2)
    return x

_drawn_inputs = setup_inputs


def setup_inputs(seed=0):
    import zlib

    import numpy as np

    out = dict(_drawn_inputs(seed))
    spreads = {'L0_attn_b1q': (0.0, 0.1),
     'L0_attn_b2q': (0.0, 0.1),
     'L0_attn_b1k': (0.0, 0.1),
     'L0_attn_b2k': (0.0, 0.1),
     'L0_attn_b1v': (0.0, 0.1),
     'L0_attn_b2v': (0.0, 0.1),
     'L0_attn_ln_w': (1.0, 0.2),
     'L0_attn_ln_b': (0.0, 0.1),
     'L0_xattn_ln_w': (1.0, 0.6),
     'L0_xattn_ln_b': (0.0, 0.8)}
    factors = {'ctx_1024': 2.843,
     'L0_attn_W1v': 3.607,
     'L0_xattn_Wq': 8.0,
     'L0_xattn_Wkv': 2.788,
     'L0_xattn_Wout': 2.877,
     'L0_ffn_gate_w': 8.0,
     'L0_ffn_w1': 7.18,
     'L0_ffn_w3': 7.139,
     'L0_ffn_w2': 7.132}
    for name, (base, spread) in spreads.items():
        noise = np.random.default_rng([zlib.crc32(name.encode()), seed]).standard_normal(out[name].shape)
        drawn = base * np.exp(spread * noise) if base else spread * noise
        out[name] = jnp.asarray(drawn.astype(out[name].dtype))
    for name, factor in factors.items():
        out[name] = (out[name] * factor).astype(out[name].dtype)
    return out
```

```python
from contextlib import ExitStack

import concourse.bass as bass
from concourse import mybir

ALU = mybir.AluOpType
ACT = mybir.ActivationFunctionType
AX = mybir.AxisListType
F32 = mybir.dt.float32
F16 = mybir.dt.float16
BF16 = mybir.dt.bfloat16
I32 = mybir.dt.int32
U32 = mybir.dt.uint32

BATCH, SEQ, C = 8, 56, 128
NV = 1500
NB = 4
TB = BATCH * SEQ // NB
NT = BATCH * SEQ
H, DH = 8, 64
KS = 5
GT = 16
GB = TB // GT
G = NB * GB
GR = GT * KS
E, F = 8, 512
FC = F // 128
EPS = 1e-5
SCORE_SCALE = float((128.0 * 256.0) ** 0.5)
CG = 6
CHUNKS = [(a, min(a + CG, G)) for a in range(0, G, CG)]
QG = 4
QUADS = G // QG


def decoder_layer(nc, x, ctx_rows, mask, w_attn, cols, rows, w_x, w_gate, w_ffn, consts, selector, out):
    with ExitStack() as stack:
        def sb(name, shape, dt=F32):
            return stack.enter_context(nc.sbuf_tensor(name, shape, dt))

        def sem(name):
            return stack.enter_context(nc.semaphore(name))

        bank = [stack.enter_context(nc.psum_tensor(f"bank{i}", [128, 512], F32)) for i in range(8)]

        x_tok = sb("x_tok", [TB, NB, C])
        arena = sb("arena", [128, NB * NV])
        mask_sb = arena[0:TB, :].bitcast(I32).rearrange("p (b v) -> p b v", b=NB)
        wa = sb("wa", [128, 6, C])
        col = sb("col", [128, 7])
        row = sb("row", [TB, 3, C])
        wx = sb("wx", [128, 4, 4, C])
        gate = sb("gate", [C, E])
        wf = sb("wf", [128, E, 3, F])
        cst = sb("cst", [128, 128 + TB + GT + G + E])
        sel = sb("sel", [3 * E, E, 128], BF16)
        ident = cst[:, 0:128]
        causal = cst[0:TB, 128:128 + TB]
        own = cst[:, 128 + TB:128 + TB + GT]
        row_base = cst[0:GR, 128 + TB + GT:128 + TB + GT + G]
        expert_no = cst[0:TB, 128 + TB + GT + G:128 + TB + GT + G + E]

        key_w = sb("key_w", [TB, NV])
        keys = sb("keys", [128, 2, NV])
        key = keys[0:TB, :, :]
        top = sb("top", [TB, NB, 8], F16)
        ident16 = sb("ident16", [TB, TB], F16)
        rep16 = sb("rep16", [TB, GB, H, GT], F16)
        identb = sb("identb", [TB, TB], BF16)
        ones16 = sb("ones16", [TB, 1], F16)
        spread = sb("spread", [TB, 2, TB, KS], F16)
        ridx = sb("ridx", [GR, G])
        row_idx = sb("row_idx", [GR, G], I32)
        vg = sb("vg", [GR, G, C])
        vgT = sb("vgT", [C, G, GR])
        keyrep = sb("keyrep", [128, GB, NB, KS])
        valid = sb("valid", [128, G, KS])
        vbias = sb("vbias", [128, G, KS])
        mhalf = sb("mhalf", [TB, NB])
        eps = sb("eps", [TB, NB])

        stats = sb("stats", [TB, NB, 6])
        mv = sb("mv", [TB, NB, 2])
        ve = sb("ve", [TB, NB])
        rstd = sb("rstd", [TB, NB])
        r2 = sb("r2", [TB, NB])
        vr = sb("vr", [TB, NB])
        vr2 = sb("vr2", [TB, NB])
        xn = sb("xn", [TB, NB, C])
        xnT = sb("xnT", [C, NT])
        hid = sb("hid", [C, 3, NT])
        qT = sb("qT", [C, NT])
        kT = sb("kT", [C, NT])
        v_tok = sb("v_tok", [TB, NB, C])
        sT = sb("sT", [TB, NB, TB])
        on = sb("on", [TB, NB, C])
        onw = on
        xb = sb("xb", [TB, NB, C])
        x1 = sb("x1", [TB, NB, C])
        aw = sb("aw", [C, H, C])
        mw = sb("mw", [C, H, C])
        qp = sb("qp", [C, G, H, GT])
        simx = keys[:, :, 0:CG * GR].rearrange("p s (g t k) -> p s g t k", t=GT, k=KS)
        sim = sb("sim", [128, G, KS])
        s1 = sb("s1", [128, G, KS])
        s2 = sb("s2", [128, G, KS])
        s3 = sb("s3", [128, G, KS])
        ex = sb("ex", [128, G, KS])
        exv = sb("exv", [128, G, KS])
        smax = sb("smax", [128, G])
        ssum = sb("ssum", [128, G])
        srec = sb("srec", [128, G])
        attn = sb("attn", [128, G, KS])
        attT = arena[0:GR, 0:G * 128].rearrange("p (g r) -> p g r", g=G)
        attx = arena[:, G * 128:G * (128 + GR)].rearrange("p (g t k) -> p g t k", g=G, k=KS)
        cxT = sb("cxT", [C, H, NT])
        x2 = sb("x2", [TB, NB, C])
        lmax = sb("lmax", [TB, NB])
        ld = sb("ld", [TB, NB, E])
        le = sb("le", [TB, NB, E])
        ltop = sb("ltop", [TB, NB, 8])
        lidx = sb("lidx", [TB, NB, 8], U32)
        lidf = sb("lidf", [TB, NB, 2])
        lsum = sb("lsum", [TB, NB])
        lrec = sb("lrec", [TB, NB])
        lw = sb("lw", [TB, NB, 2])
        pick = sb("pick", [TB, NB, 2, E])
        pickw = sb("pickw", [TB, NB, 2, E])
        wi = sb("wi", [TB, NB, E])
        wi1 = sb("wi1", [TB, NB, E])
        wi2 = sb("wi2", [TB, NB, E])
        wparts = sb("wparts", [TB, NB, 3, E], BF16)
        wT = sb("wT", [3 * E, NT], BF16)
        NS = 3
        qflat = qp[:, :, :, :].rearrange("p g h t -> p (g h t)").rearrange("p (s n) -> p s n", n=NT)
        sil, silw, wb = qflat[:, 0:NS, :], qflat[:, NS:2 * NS, :], qflat[:, 2 * NS:2 * NS + 2, :]
        hh = vgT[:, :, :].rearrange("p g r -> p (g r)")[:, 0:NS * NT].rearrange("p (s n) -> p s n", s=NS)
        yT = sb("yT", [C, NT])
        y_out = x1

        x_in = sem("x_in")
        cst_in = sem("cst_in")
        wa_in = sem("wa_in")
        col_in = sem("col_in")
        row_in = sem("row_in")
        mask_in = [sem(f"mask_in{b}") for b in range(NB)]
        wx_in = sem("wx_in")
        gate_in = sem("gate_in")
        sel_in = sem("sel_in")
        wf_in = [sem(f"wf_in{e}") for e in range(E)]
        rows_in = [sem(f"rows_in{c}") for c in range(len(CHUNKS))]
        y_stored = sem("y_stored")
        keyw_ready = sem("keyw_ready")
        small_ready = sem("small_ready")
        key_ready = sem("key_ready")
        top_ready = sem("top_ready")
        spread_ready = sem("spread_ready")
        idx_ps = sem("idx_ps")
        idx_ready = sem("idx_ready")
        keyrep_ps = sem("keyrep_ps")
        keyrep_read = sem("keyrep_read")
        vgT_ps = sem("vgT_ps")
        vgT_ready = sem("vgT_ready")
        var_ready = sem("var_ready")
        rstd_ready = sem("rstd_ready")
        xn_ready = sem("xn_ready")
        xnT_ps = sem("xnT_ps")
        xnT_ready = sem("xnT_ready")
        h_ps = sem("h_ps")
        hid_ready = sem("hid_ready")
        qkv_ps = sem("qkv_ps")
        qkv_ready = sem("qkv_ready")
        s_ps = sem("s_ps")
        sT_ready = sem("sT_ready")
        o_ps = sem("o_ps")
        wh_ps = sem("wh_ps")
        wh_ready = sem("wh_ready")
        qp_ps = sem("qp_ps")
        qp_act = sem("qp_act")
        qp_dve = sem("qp_dve")
        sim_ps = sem("sim_ps")
        sim_read = sem("sim_read")
        sim_summed = sem("sim_summed")
        s3_ready = sem("s3_ready")
        ex_ready = sem("ex_ready")
        attx_ready = sem("attx_ready")
        attT_ps = sem("attT_ps")
        attT_ready = sem("attT_ready")
        cx_ps = sem("cx_ps")
        cx_ready = sem("cx_ready")
        xo_ps = sem("xo_ps")
        logit_ps = sem("logit_ps")
        ld_ready = sem("ld_ready")
        le_ready = sem("le_ready")
        wparts_ready = sem("wparts_ready")
        wT_ps = sem("wT_ps")
        wT_ready = sem("wT_ready")
        wb_ps = sem("wb_ps")
        wb_ready = sem("wb_ready")
        up_ps = sem("up_ps")
        sil_ready = sem("sil_ready")
        silw_ready = sem("silw_ready")
        hh_ready = sem("hh_ready")
        down_done = sem("down_done")
        yT_ready = sem("yT_ready")
        y_ps = sem("y_ps")
        y_ready = sem("y_ready")
        dve_done = sem("dve_done")
        pool_done = sem("pool_done")

        NCH = E * FC
        BX = [bank[0], bank[1], bank[4], bank[5]]
        BV = [bank[2], bank[3]]
        BS = [bank[2], bank[3], bank[6]]
        BA = [bank[0], bank[1]]
        BC = [bank[4], bank[5]]
        UP1 = [bank[3], bank[4]]
        UP3 = [bank[0], bank[1], bank[6]]
        Y = bank[7]

        block = stack.enter_context(nc.Block())

        @block.sync
        def _(sp):
            sp.dma_start(x_tok[:, :, :], x.rearrange("(b p) c -> p b c", p=TB)).then_inc(x_in, 16)
            sp.dma_start(wa[:, :, :], w_attn).then_inc(wa_in, 16)
            for b in range(NB):
                sp.dma_start(mask_sb[:, b, :], mask[b]).then_inc(mask_in[b], 16)
            sp.dma_start(wx[:, :, :, :], w_x).then_inc(wx_in, 16)
            sp.dma_start(gate[:, :], w_gate).then_inc(gate_in, 16)
            sp.dma_start(sel[:, :, :], selector).then_inc(sel_in, 16)
            for e in range(E):
                sp.dma_start(wf[:, e, :, :], w_ffn[e]).then_inc(wf_in[e], 16)
            sp.wait_ge(y_ready, 1)
            sp.dma_start(out.rearrange("(b p) c -> p b c", p=TB), y_out[:, :, :]).then_inc(y_stored, 16)
            sp.wait_ge(y_stored, 16)

        @block.gpsimd
        def _(pool):
            pool.memset(mhalf[:, :], -0.5)
            pool.memset(ones16[:, :], 1.0).then_inc(small_ready, 1)
            pool.iota(key_w[:, :], [[-1, NV]], base=NV, channel_multiplier=0,
                      allow_small_or_imprecise_dtypes=True).then_inc(keyw_ready, 1)
            pool.wait_ge(cst_in, 16)
            pool.tensor_copy(ident16[:, :], ident[0:TB, 0:TB]).then_inc(small_ready, 1)
            pool.tensor_copy(identb[:, :], ident[0:TB, 0:TB]).then_inc(small_ready, 1)
            for i in range(GB):
                last = pool.tensor_copy(rep16[:, i, :, :], ident[0:TB, i * GT:(i + 1) * GT].unsqueeze(1)
                                        .broadcast_to([TB, H, GT]))
            last.then_inc(small_ready, 1)

            def rsqrt(n):
                if n == 0:
                    pool.wait_ge(small_ready, 1)
                pool.wait_ge(var_ready, n + 1)
                pool.tensor_tensor(rstd[:, :], ve[:, :], mhalf[:, :], ALU.pow).then_inc(rstd_ready, 1)

            def spread_keys(b):
                pool.wait_ge(top_ready, b + 1)
                pool.wait_ge(small_ready, 3)
                if b >= 2:
                    pool.wait_ge(idx_ps, b - 1)
                pool.tensor_tensor(spread[:, b % 2, :, :],
                                   ident16[:, :].unsqueeze(2).broadcast_to([TB, TB, KS]),
                                   top[:, b, 0:KS].unsqueeze(1).broadcast_to([TB, TB, KS]),
                                   ALU.mult).then_inc(spread_ready, 1)

            def gather(b):
                pool.wait_ge(idx_ready, b + 1)
                for g in range(b * GB, (b + 1) * GB):
                    pool.indirect_dma_start(
                        out=vg[:, g, :], out_offset=None, in_=ctx_rows,
                        in_offset=bass.IndirectOffsetOnAxis(ap=row_idx[:, g:g + 1], axis=0),
                    ).then_inc(rows_in[g // CG], 16)

            rsqrt(0)
            for b in range(2):
                spread_keys(b)
                gather(b)
            rsqrt(1)
            rsqrt(2)
            rsqrt(3)
            for b in range(2, NB):
                spread_keys(b)
                gather(b)
            rsqrt(4)
            for i in range(NCH):
                e = i // FC
                pool.wait_ge(sil_ready, i + 1)
                pool.wait_ge(wb_ready, e + 1)
                if i >= NS:
                    pool.wait_ge(hh_ready, i - NS + 1)
                pool.tensor_tensor(silw[:, i % NS, :], sil[:, i % NS, :], wb[:, e % 2, :],
                                   ALU.mult).then_inc(silw_ready, 1)

        @block.scalar
        def _(act):
            act.dma_start(cst[:, :], consts).then_inc(cst_in, 16)
            act.dma_start(col[:, :], cols).then_inc(col_in, 16)
            act.dma_start(row[:, :, :], rows.partition_broadcast(TB)).then_inc(row_in, 16)
            act.wait_ge(xnT_ps, 1)
            act.copy(xnT[:, :], bank[0][:, 0:NT]).then_inc(xnT_ready, 1)
            act.wait_ge(col_in, 16)
            for n in range(3):
                act.wait_ge(h_ps, n + 1)
                act.activation(hid[:, n, :], bank[1 + n][:, 0:NT], ACT.Gelu,
                               bias=col[:, n:n + 1]).then_inc(hid_ready, 1)
            act.wait_ge(xnT_ps, 2)
            act.activation(xnT[:, :], bank[0][:, 0:NT], ACT.Identity, bias=col[:, 6:7],
                           scale=col[:, 5:6]).then_inc(xnT_ready, 1)
            for h in range(0, H, 2):
                act.wait_ge(qp_ps, h + 1)
                act.copy(qp[:, :, h, :], BX[h % 4][:, 0:NT].rearrange("p (g t) -> p g t", t=GT)).then_inc(qp_act, 1)
            for c, (a, z) in enumerate(CHUNKS):
                act.wait_ge(vgT_ps, c + 1)
                act.copy(vgT[:, a:z, :].rearrange("p g r -> p (g r)"),
                         BV[c % 2][:, 0:(z - a) * GR]).then_inc(vgT_ready, 1)
            act.wait_ge(s3_ready, 1)
            act.activation(ex[:, :, :], s3[:, :, :], ACT.Exp).then_inc(ex_ready, 1)
            for q in range(QUADS):
                act.wait_ge(attT_ps, q + 1)
                act.copy(attT[:, q * QG:(q + 1) * QG, :].rearrange("p g r -> p (g r)"),
                         BA[q % 2][0:GR, :]).then_inc(attT_ready, 1)
            act.wait_ge(xnT_ps, 3)
            act.copy(xnT[:, :], bank[0][:, 0:NT]).then_inc(xnT_ready, 1)
            act.wait_ge(ld_ready, 1)
            act.activation(le[:, :, :], ld[:, :, :], ACT.Exp).then_inc(le_ready, 1)

            def weight_copy(e):
                act.wait_ge(wb_ps, e + 1)
                if e >= 2:
                    act.wait_ge(silw_ready, FC * (e - 1))
                act.copy(wb[:, e % 2, :], bank[2][:, 0:NT]).then_inc(wb_ready, 1)

            for i in range(NCH):
                act.wait_ge(up_ps, 2 * i + 1)
                if i >= NS:
                    act.wait_ge(silw_ready, i - NS + 1)
                act.activation(sil[:, i % NS, :], UP1[i % 2][:, 0:NT], ACT.Silu).then_inc(sil_ready, 1)
                if i % FC == 0:
                    weight_copy(i // FC)

        @block.vector
        def _(dve):
            chain = [0]

            def then(ins):
                chain[0] += 1
                ins.then_inc(dve_done, 1)
                dve.wait_ge(dve_done, chain[0])

            def find_rows(b):
                dve.wait_ge(mask_in[b], 16)
                if b == 0:
                    dve.wait_ge(keyw_ready, 1)
                then(dve.scalar_tensor_tensor(out=key[:, b % 2, :], in0=mask_sb[:, b, :], scalar=0.0,
                                              in1=key_w[:, :], op0=ALU.not_equal, op1=ALU.mult))
                dve.max(top[:, b, :], key[:, b % 2, :]).then_inc(top_ready, 1)

            def index_rows(b):
                g0, g1 = b * GB, (b + 1) * GB
                dve.wait_ge(idx_ps, b + 1)
                if b == 0:
                    dve.wait_ge(cst_in, 16)
                then(dve.tensor_tensor(ridx[:, g0:g1], row_base[:, g0:g1], bank[7][0:GR, g0:g1],
                                       ALU.subtract))
                dve.tensor_scalar(row_idx[:, g0:g1], ridx[:, g0:g1], float(BATCH * NV - 1), None,
                                  ALU.min).then_inc(idx_ready, 1)

            def variance(src):
                for b in range(NB):
                    last = dve.bn_stats(stats[:, b, :], src[:, b, :])
                then(last)
                for b in range(NB):
                    last = dve.bn_aggr(mv[:, b, :], stats[:, b, :])
                then(last)
                dve.tensor_scalar(ve[:, :], mv[:, :, 1], EPS, None, ALU.add).then_inc(var_ready, 1)

            def normalise(dst, src, scale):
                for b in range(NB):
                    last = dve.tensor_scalar(dst[:, b, :], src[:, b, :], mv[:, b, 0:1], scale[:, b:b + 1],
                                             ALU.subtract, ALU.mult)
                return last

            def blocks(ap, n):
                return ap.unsqueeze(1).broadcast_to([ap.shape[0], n, ap.shape[1]])

            dve.wait_ge(x_in, 16)
            variance(x_tok)
            dve.wait_ge(rstd_ready, 1)
            normalise(xn, x_tok, rstd).then_inc(xn_ready, 1)
            dve.wait_ge(row_in, 16)
            dve.tensor_tensor(xb[:, :, :], x_tok[:, :, :], blocks(row[:, 2, :], NB), ALU.add)
            find_rows(0)
            dve.wait_ge(col_in, 16)
            dve.wait_ge(qkv_ps, 1)
            dve.tensor_scalar(qT[:, :], bank[4][:, 0:NT], col[:, 3:4], None, ALU.add).then_inc(qkv_ready, 1)
            dve.wait_ge(qkv_ps, 2)
            dve.tensor_scalar(kT[:, :], bank[5][:, 0:NT], col[:, 4:5], None, ALU.add).then_inc(qkv_ready, 1)
            dve.wait_ge(qkv_ps, 3)
            dve.tensor_tensor(v_tok[:, :, :], bank[6][0:TB, :].rearrange("p (b c) -> p b c", b=NB),
                              blocks(row[:, 0, :], NB), ALU.add).then_inc(qkv_ready, 1)
            index_rows(0)
            dve.wait_ge(s_ps, 1)
            dve.tensor_tensor(sT[:, :, :], bank[0][0:TB, 0:NB * TB].rearrange("p (b c) -> p b c", b=NB),
                              blocks(causal, NB), ALU.mult).then_inc(sT_ready, 1)
            find_rows(1)
            dve.wait_ge(o_ps, 1)
            o_tok = bank[1][0:TB, :].rearrange("p (b c) -> p b c", b=NB)
            variance(o_tok)
            index_rows(1)
            dve.wait_ge(rstd_ready, 2)
            then(normalise(on, o_tok, rstd))
            then(dve.tensor_tensor(onw[:, :, :], on[:, :, :], blocks(row[:, 1, :], NB), ALU.mult))
            then(dve.tensor_tensor(x1[:, :, :], onw[:, :, :], xb[:, :, :], ALU.add))
            variance(x1)
            dve.wait_ge(rstd_ready, 3)
            then(dve.tensor_copy(r2[:, :], rstd[:, :]))
            then(dve.tensor_tensor(vr[:, :], mv[:, :, 1], r2[:, :], ALU.mult))
            then(dve.tensor_tensor(vr2[:, :], vr[:, :], r2[:, :], ALU.mult))
            dve.tensor_scalar(ve[:, :], vr2[:, :], EPS, None, ALU.add).then_inc(var_ready, 1)
            dve.wait_ge(rstd_ready, 4)
            then(dve.tensor_tensor(vr[:, :], rstd[:, :], r2[:, :], ALU.mult))
            normalise(xn, x1, vr).then_inc(xn_ready, 1)
            find_rows(2)
            find_rows(3)
            for n in range(4):
                dve.wait_ge(wh_ps, n + 1)
                dst, scale = (aw, DH ** -0.5) if n < 2 else (mw, 1.0)
                dve.tensor_scalar(dst[:, n % 2:H:2, :],
                                  [bank[4], bank[5]][n % 2][:, :].rearrange("p (j c) -> p j c", c=C), scale, None,
                                  ALU.mult).then_inc(wh_ready, 1)
            index_rows(2)
            index_rows(3)
            for h in range(1, H, 2):
                dve.wait_ge(qp_ps, h + 1)
                dve.tensor_copy(qp[:, :, h, :], BX[h % 4][:, 0:NT].rearrange("p (g t) -> p g t", t=GT)).then_inc(qp_dve, 1)
            dve.wait_ge(keyrep_ps, 1)
            dve.tensor_copy(keyrep[:, :, :, :].rearrange("p i b k -> p (i b k)"),
                            bank[7][:, 128:128 + GB * NB * KS]).then_inc(keyrep_read, 1)
            dve.wait_ge(keyrep_read, 1)
            then(dve.tensor_scalar(valid[:, :, :].rearrange("p (b i) k -> p b i k", b=NB),
                                   keyrep[:, :, :, :].rearrange("p i b k -> p b i k"), 1.0, None, ALU.min))
            dve.tensor_scalar(vbias[:, :, :], valid[:, :, :], 10000.0, -10000.0, ALU.mult, ALU.add)
            for c in range(len(CHUNKS) + 1):
                if c < len(CHUNKS):
                    a, z = CHUNKS[c]
                    dve.wait_ge(sim_ps, c + 1)
                    if c >= 2:
                        dve.wait_ge(sim_summed, c - 1)
                    dve.tensor_tensor(simx[:, c % 2, 0:z - a, :, :],
                                      BS[c % 3][:, 0:(z - a) * GR].rearrange("p (g t k) -> p g t k", t=GT, k=KS),
                                      own.unsqueeze(1).unsqueeze(3).broadcast_to([128, z - a, GT, KS]),
                                      ALU.mult).then_inc(sim_read, 1)
                if c >= 1:
                    a, z = CHUNKS[c - 1]
                    dve.wait_ge(sim_read, c)
                    dve.tensor_reduce(sim[:, a:z, :],
                                      simx[:, (c - 1) % 2, 0:z - a, :, :].rearrange("p g t k -> p g k t"),
                                      AX.X, ALU.add).then_inc(sim_summed, 1)
            dve.wait_ge(sim_summed, len(CHUNKS))
            then(dve.tensor_tensor(s1[:, :, :], sim[:, :, :], valid[:, :, :], ALU.mult))
            then(dve.tensor_tensor(s2[:, :, :], s1[:, :, :], vbias[:, :, :], ALU.add))
            then(dve.tensor_reduce(smax[:, :], s2[:, :, :], AX.X, ALU.max))
            dve.tensor_tensor(s3[:, :, :], s2[:, :, :], smax[:, :].unsqueeze(2).broadcast_to([128, G, KS]),
                              ALU.subtract).then_inc(s3_ready, 1)
            dve.wait_ge(ex_ready, 1)
            then(dve.tensor_reduce(ssum[:, :], ex[:, :, :], AX.X, ALU.add))
            dve.reciprocal(srec[:, :], ssum[:, :])
            then(dve.tensor_tensor(exv[:, :, :], ex[:, :, :], valid[:, :, :], ALU.mult))
            then(dve.tensor_tensor(attn[:, :, :], exv[:, :, :],
                                   srec[:, :].unsqueeze(2).broadcast_to([128, G, KS]), ALU.mult))
            for q in range(QUADS):
                g0, g1 = q * QG, (q + 1) * QG
                dve.tensor_tensor(attx[:, g0:g1, :, :],
                                  attn[:, g0:g1, :].unsqueeze(2).broadcast_to([128, QG, GT, KS]),
                                  own.unsqueeze(1).unsqueeze(3).broadcast_to([128, QG, GT, KS]),
                                  ALU.mult).then_inc(attx_ready, 1)
            for q in range(QUADS):
                t0, t1 = q * QG * GT, (q + 1) * QG * GT
                dve.wait_ge(cx_ps, q + 1)
                dve.tensor_copy(cxT[:, :, t0:t1].rearrange("p h (g t) -> p g h t", t=GT),
                                BC[q % 2][:, :].rearrange("p (g h t) -> p g h t", h=H, t=GT)
                                ).then_inc(cx_ready, 1)
            dve.wait_ge(xo_ps, 1)
            then(dve.tensor_tensor(x2[:, :, :], x1[:, :, :],
                                   bank[7][0:TB, :].rearrange("p (b c) -> p b c", b=NB), ALU.add))
            variance(x2)
            dve.wait_ge(rstd_ready, 5)
            normalise(xn, x2, rstd).then_inc(xn_ready, 1)
            dve.wait_ge(logit_ps, 1)
            logits = bank[1][0:TB, 0:NB * E].rearrange("p (b e) -> p b e", b=NB)
            then(dve.tensor_reduce(lmax[:, :], logits, AX.X, ALU.max))
            dve.tensor_tensor(ld[:, :, :], logits, lmax[:, :].unsqueeze(2).broadcast_to([TB, NB, E]),
                              ALU.subtract).then_inc(ld_ready, 1)
            dve.wait_ge(le_ready, 1)
            for b in range(NB):
                last = dve.max(ltop[:, b, :], le[:, b, :])
            then(last)
            for b in range(NB):
                last = dve.max_index(lidx[:, b, :], ltop[:, b, :], le[:, b, :])
            then(dve.tensor_tensor(lsum[:, :], ltop[:, :, 0], ltop[:, :, 1], ALU.add))
            then(dve.reciprocal(lrec[:, :], lsum[:, :]))
            dve.tensor_tensor(lw[:, :, :], ltop[:, :, 0:2],
                              lrec[:, :].unsqueeze(2).broadcast_to([TB, NB, 2]), ALU.mult)
            then(dve.tensor_copy(lidf[:, :, :], lidx[:, :, 0:2]))
            then(dve.tensor_tensor(pick[:, :, :, :],
                                   expert_no.unsqueeze(1).unsqueeze(1).broadcast_to([TB, NB, 2, E]),
                                   lidf[:, :, :].unsqueeze(3).broadcast_to([TB, NB, 2, E]), ALU.is_equal))
            then(dve.tensor_tensor(pickw[:, :, :, :], pick[:, :, :, :],
                                   lw[:, :, :].unsqueeze(3).broadcast_to([TB, NB, 2, E]), ALU.mult))
            then(dve.tensor_tensor(wi[:, :, :], pickw[:, :, 0, :], pickw[:, :, 1, :], ALU.add))
            then(dve.tensor_copy(wparts[:, :, 0, :], wi[:, :, :]))
            then(dve.tensor_tensor(wi1[:, :, :], wi[:, :, :], wparts[:, :, 0, :], ALU.subtract))
            then(dve.tensor_copy(wparts[:, :, 1, :], wi1[:, :, :]))
            then(dve.tensor_tensor(wi2[:, :, :], wi1[:, :, :], wparts[:, :, 1, :], ALU.subtract))
            dve.tensor_copy(wparts[:, :, 2, :], wi2[:, :, :]).then_inc(wparts_ready, 1)
            dve.wait_ge(wT_ps, 1)
            dve.tensor_copy(wT[:, :], bank[5][0:3 * E, 0:NT // 2].bitcast(BF16)).then_inc(wT_ready, 1)
            for i in range(NCH):
                dve.wait_ge(up_ps, 2 * i + 2)
                dve.wait_ge(silw_ready, i + 1)
                if i >= NS:
                    dve.wait_ge(down_done, i - NS + 1)
                dve.tensor_tensor(hh[:, i % NS, :], silw[:, i % NS, :], UP3[i % 3][:, 0:NT],
                                  ALU.mult).then_inc(hh_ready, 1)
            dve.wait_ge(down_done, NCH)
            dve.tensor_copy(yT[:, :], Y[:, 0:NT]).then_inc(yT_ready, 1)
            dve.wait_ge(y_ps, 1)
            dve.tensor_tensor(y_out[:, :, :], x2[:, :, :],
                              bank[2][0:TB, :].rearrange("p (b c) -> p b c", b=NB),
                              ALU.add).then_inc(y_ready, 1)

        @block.tensor
        def _(pe):
            def turn_tokens(n, dst):
                pe.wait_ge(xn_ready, n + 1)
                if n == 0:
                    pe.wait_ge(cst_in, 16)
                for b in range(NB):
                    last = pe.transpose(dst[:, b * TB:(b + 1) * TB], xn[:, b, :], ident[0:TB, 0:TB])
                last.then_inc(xnT_ps, 1)

            def place_keys(b):
                pe.wait_ge(spread_ready, b + 1)
                if b >= 1:
                    pe.wait_ge(idx_ready, b)
                for i in range(GB):
                    last = pe.matmul(bank[7][0:GR, b * GB + i:b * GB + i + 1],
                                     spread[:, b % 2, i * GT:(i + 1) * GT, :], ones16[:, :],
                                     start=True, stop=True)
                last.then_inc(idx_ps, 1)

            turn_tokens(0, bank[0])
            pe.wait_ge(wa_in, 16)
            pe.wait_ge(xnT_ready, 1)
            for n in range(3):
                pe.matmul(bank[1 + n][:, 0:NT], wa[:, n, :], xnT[:, :], start=True, stop=True).then_inc(h_ps, 1)
            for n in range(2):
                pe.wait_ge(hid_ready, n + 1)
                pe.matmul(bank[4 + n][:, 0:NT], wa[:, 3 + n, :], hid[:, n, :],
                          start=True, stop=True).then_inc(qkv_ps, 1)
            pe.wait_ge(hid_ready, 3)
            for b in range(NB):
                last = pe.matmul(bank[6][0:TB, b * C:(b + 1) * C], hid[:, 2, b * TB:(b + 1) * TB],
                                 wa[:, 5, :], start=True, stop=True)
            last.then_inc(qkv_ps, 1)
            place_keys(0)
            pe.wait_ge(qkv_ready, 2)
            for b in range(NB):
                t = slice(b * TB, (b + 1) * TB)
                last = pe.matmul(bank[0][0:TB, t], kT[:, t], qT[:, t], start=True, stop=True)
            last.then_inc(s_ps, 1)
            pe.wait_ge(wx_in, 16)

            def head_weights(n):
                if n >= 2:
                    pe.wait_ge(wh_ready, n - 1)
                for j in range(4):
                    p = slice(DH * (n % 2), DH * (n % 2) + DH)
                    last = pe.matmul([bank[4], bank[5]][n % 2][:, j * C:(j + 1) * C],
                                     wx[p, 2 * (n // 2), j, :], wx[p, 2 * (n // 2) + 1, j, :],
                                     start=True, stop=True)
                last.then_inc(wh_ps, 1)

            pe.wait_ge(sT_ready, 1)
            pe.wait_ge(qkv_ready, 3)
            for b in range(NB):
                last = pe.matmul(bank[1][0:TB, b * C:(b + 1) * C], sT[:, b, :], v_tok[:, b, :],
                                 start=True, stop=True)
            last.then_inc(o_ps, 1)
            place_keys(1)
            for n in range(2):
                head_weights(n)
            turn_tokens(1, bank[0])
            for n in range(2, 4):
                head_weights(n)
            place_keys(2)
            place_keys(3)
            pe.wait_ge(idx_ready, 4)
            pe.wait_ge(small_ready, 4)
            for i in range(GB):
                last = pe.matmul(bank[7][:, 128 + i * NB * KS:128 + (i + 1) * NB * KS],
                                 rep16[:, i, :, :].rearrange("p h t -> p (h t)"),
                                 top[:, :, 0:KS], start=True, stop=True)
            last.then_inc(keyrep_ps, 1)
            pe.wait_ge(xnT_ready, 2)
            pe.wait_ge(wh_ready, 4)
            for h in range(H):
                if h >= 4:
                    pe.wait_ge(qp_dve if h % 2 else qp_act, (h - 4) // 2 + 1)
                pe.matmul(BX[h % 4][:, 0:NT], aw[:, h, :], xnT[:, :], start=True, stop=True).then_inc(qp_ps, 1)
            for c, (a, z) in enumerate(CHUNKS):
                pe.wait_ge(rows_in[c], 16 * (z - a))
                if c >= 2:
                    pe.wait_ge(vgT_ready, c - 1)
                for g in range(a, z):
                    last = pe.transpose(BV[c % 2][:, (g - a) * GR:(g - a + 1) * GR], vg[:, g, :],
                                        ident[0:GR, 0:GR])
                last.then_inc(vgT_ps, 1)
            pe.wait_ge(qp_act, 4)
            pe.wait_ge(qp_dve, 4)
            for c, (a, z) in enumerate(CHUNKS):
                pe.wait_ge(vgT_ready, max(c + 1, 5 if c < 2 else 0))
                if c >= 3:
                    pe.wait_ge(sim_read, c - 2)
                for g in range(a, z):
                    last = pe.matmul(BS[c % 3][:, (g - a) * GR:(g - a + 1) * GR],
                                     qp[:, g, :, :].rearrange("p h t -> p (h t)"), vgT[:, g, :], start=True, stop=True)
                last.then_inc(sim_ps, 1)
            for q in range(QUADS + 1):
                if q < QUADS:
                    pe.wait_ge(attx_ready, q + 1)
                    if q >= 2:
                        pe.wait_ge(attT_ready, q - 1)
                    for j in range(QG):
                        last = pe.transpose(BA[q % 2][0:GR, j * 128:(j + 1) * 128],
                                            attx[:, q * QG + j, :, :].rearrange("p t k -> p (t k)"), ident)
                    last.then_inc(attT_ps, 1)
                if q >= 1:
                    pe.wait_ge(attT_ready, q)
                    if q >= 3:
                        pe.wait_ge(cx_ready, q - 2)
                    for j in range(QG):
                        g = (q - 1) * QG + j
                        last = pe.matmul(BC[(q - 1) % 2][:, j * 128:(j + 1) * 128], vg[:, g, :], attT[:, g, :],
                                         start=True, stop=True)
                    last.then_inc(cx_ps, 1)
            pe.wait_ge(cx_ready, QUADS)
            pe.wait_ge(keyrep_read, 1)
            for b in range(NB):
                for h in range(H):
                    last = pe.matmul(bank[7][0:TB, b * C:(b + 1) * C], cxT[:, h, b * TB:(b + 1) * TB],
                                     mw[:, h, :], start=(h == 0), stop=(h == H - 1))
            last.then_inc(xo_ps, 1)
            turn_tokens(2, bank[0])
            pe.wait_ge(xnT_ready, 3)
            pe.wait_ge(gate_in, 16)
            for b in range(NB):
                last = pe.matmul(bank[1][0:TB, b * E:(b + 1) * E], xnT[:, b * TB:(b + 1) * TB], gate[:, :],
                                 start=True, stop=True)
            last.then_inc(logit_ps, 1)

            def up(i):
                e, c = i // FC, i % FC
                if c == 0:
                    pe.wait_ge(wf_in[e], 16)
                if i >= 2:
                    pe.wait_ge(sil_ready, i - 1)
                pe.matmul(UP1[i % 2][:, 0:NT], wf[:, e, 0, c * 128:(c + 1) * 128], xnT[:, :],
                          start=True, stop=True).then_inc(up_ps, 1)
                if i >= 3:
                    pe.wait_ge(hh_ready, i - 2)
                if i == 1:
                    pe.wait_ge(ld_ready, 1)
                pe.matmul(UP3[i % 3][:, 0:NT], wf[:, e, 1, c * 128:(c + 1) * 128], xnT[:, :],
                          start=True, stop=True).then_inc(up_ps, 1)

            def down(i):
                e, c = i // FC, i % FC
                pe.wait_ge(hh_ready, i + 1)
                pe.matmul(Y[:, 0:NT], wf[:, e, 2, c * 128:(c + 1) * 128], hh[:, i % NS, :],
                          start=(i == 0), stop=(i == NCH - 1), skip_group_check=True).then_inc(down_done, 1)

            def weights_of(e):
                if e >= 1:
                    pe.wait_ge(wb_ready, e)
                pe.matmul(bank[2][:, 0:NT], sel[:, e, :], wT[:, :], start=True, stop=True).then_inc(wb_ps, 1)

            up(0)
            up(1)
            pe.wait_ge(wparts_ready, 1)
            pe.wait_ge(small_ready, 3)
            for b in range(NB):
                last = pe.transpose(bank[5][0:3 * E, b * TB // 2:(b + 1) * TB // 2].bitcast(BF16),
                                    wparts[:, b, :, :].rearrange("p a e -> p (a e)"), identb[:, :])
            last.then_inc(wT_ps, 1)
            pe.wait_ge(wT_ready, 1)
            pe.wait_ge(sel_in, 16)
            weights_of(0)
            for i in range(2, NCH + 2):
                if i < NCH:
                    up(i)
                    if i % FC == 2 and i // FC + 1 < E:
                        weights_of(i // FC + 1)
                down(i - 2)
            pe.wait_ge(yT_ready, 1)
            for b in range(NB):
                last = pe.transpose(bank[2][0:TB, b * C:(b + 1) * C], yT[:, b * TB:(b + 1) * TB], ident)
            last.then_inc(y_ps, 1)


def kernel(x, ctx_1024, mask_BxS2xS_ik0, L0_attn_W1q, L0_attn_b1q, L0_attn_W2q, L0_attn_b2q, L0_attn_W1k,
           L0_attn_b1k, L0_attn_W2k, L0_attn_b2k, L0_attn_W1v, L0_attn_b1v, L0_attn_W2v, L0_attn_b2v,
           L0_attn_ln_w, L0_attn_ln_b, L0_xattn_ln_w, L0_xattn_ln_b, L0_xattn_Wq, L0_xattn_Wkv,
           L0_xattn_Wout, L0_ffn_gate_w, L0_ffn_w1, L0_ffn_w3, L0_ffn_w2):
    import ml_dtypes
    import numpy as np
    import concourse.bacc as bacc
    from concourse.bass_utils import run_bass_kernel_spmd

    a = np.asarray
    INNER = H * DH

    def by_heads(w):
        return a(w).reshape(H // 2, 2 * DH, C).transpose(1, 0, 2)

    wkv = a(L0_xattn_Wkv)
    consts = np.zeros((128, 128 + TB + GT + G + E), np.float32)
    consts[:, 0:128] = np.eye(128)
    j, i = np.arange(TB)[:, None], np.arange(TB)[None, :]
    consts[0:TB, 128:128 + TB] = ((j <= i) & (j // SEQ == i // SEQ)) / np.float32(SCORE_SCALE)
    consts[:, 128 + TB:128 + TB + GT] = np.arange(128)[:, None] % GT == np.arange(GT)[None, :]
    token = np.arange(G)[None, :] * GT + np.arange(GR)[:, None] // KS
    consts[0:GR, 128 + TB + GT:128 + TB + GT + G] = NV * (token // SEQ + 1)
    consts[:, 128 + TB + GT + G:] = np.arange(E)
    selector = np.zeros((3 * E, E, 128), np.float32)
    for p in range(3 * E):
        selector[p, p % E] = 1.0

    arrays = {
        "x": a(x).reshape(NT, C),
        "ctx_rows": a(ctx_1024).reshape(BATCH * NV, C),
        "mask": a(mask_BxS2xS_ik0).transpose(0, 2, 1).reshape(NB, TB, NV),
        "w_attn": np.stack([a(w) for w in (L0_attn_W1q, L0_attn_W1k, L0_attn_W1v,
                                           L0_attn_W2q, L0_attn_W2k, L0_attn_W2v)], axis=1),
        "cols": np.stack([a(b) for b in (L0_attn_b1q, L0_attn_b1k, L0_attn_b1v, L0_attn_b2q, L0_attn_b2k,
                                         L0_xattn_ln_w, L0_xattn_ln_b)], axis=1),
        "rows": np.stack([a(L0_attn_b2v), a(L0_attn_ln_w), a(L0_attn_ln_b)]),
        "w_x": np.stack([by_heads(a(L0_xattn_Wq).T), by_heads(wkv[:, 0:INNER].T),
                         by_heads(wkv[:, INNER:].T), by_heads(L0_xattn_Wout)], axis=1),
        "w_gate": a(L0_ffn_gate_w),
        "w_ffn": np.stack([a(L0_ffn_w1), a(L0_ffn_w3),
                           a(L0_ffn_w2).reshape(E, FC, 128, C).transpose(0, 2, 1, 3).reshape(E, 128, F)],
                          axis=2),
        "consts": consts,
        "selector": selector.astype(ml_dtypes.bfloat16),
    }
    arrays = {name: np.ascontiguousarray(v) for name, v in arrays.items()}
    nc = bacc.Bacc("TRN2", target_bir_lowering=False, num_devices=1)
    args = [nc.dram_tensor(name, v.shape, mybir.dt.from_np(v.dtype), kind="ExternalInput").ap()
            for name, v in arrays.items()]
    out = nc.dram_tensor("out", (NT, C), F32, kind="ExternalOutput").ap()
    decoder_layer(nc, *args, out)
    r = run_bass_kernel_spmd(nc, [arrays], core_ids=[0])
    return r.results[0]["out"].reshape(BATCH, SEQ, C)
```

```python
from contextlib import ExitStack

import concourse.bass as bass
from concourse import mybir

ALU = mybir.AluOpType
ACT = mybir.ActivationFunctionType
AX = mybir.AxisListType
F32 = mybir.dt.float32
F16 = mybir.dt.float16
BF16 = mybir.dt.bfloat16
F32R = mybir.dt.float32r
I32 = mybir.dt.int32
U32 = mybir.dt.uint32

BATCH, SEQ, C = 8, 56, 128
NV = 1500
NB = 4
TB = BATCH * SEQ // NB
NT = BATCH * SEQ
H, DH = 8, 64
KS = 5
GT = 16
GB = TB // GT
G = NB * GB
GR = GT * KS
E, F = 8, 512
FC = F // 128
NCH = E * FC
WS = 6
EARLY = 5
PIECES = 8
PW = 3 * F // PIECES
NS = 4
LAG = 5
EPS = 1e-5
SCORE_SCALE = float((128.0 * 256.0) ** 0.5)
CG = 6
CHUNKS = [(a, min(a + CG, G)) for a in range(0, G, CG)]
QG = 4
QUADS = G // QG
HALVES = [(0, 2), (2, len(CHUNKS))]


def decoder_layer(nc, x, ctx_rows, mask, w_attn, cols, rows, w_x, w_gate, w_ffn, consts, out):
    with ExitStack() as stack:
        def sb(name, shape, dt=F32):
            return stack.enter_context(nc.sbuf_tensor(name, shape, dt))

        def sem(name):
            return stack.enter_context(nc.semaphore(name))

        bank = [stack.enter_context(nc.psum_tensor(f"bank{i}", [128, 512], F32)) for i in range(8)]

        col = sb("col", [128, 7])
        gate = sb("gate", [C, E])
        gate_hi = sb("gate_hi", [C, E], F32R)
        gate_lo = sb("gate_lo", [C, E], F32R)
        raw = sb("raw", [128, 2, 3 * F])
        cst = sb("cst", [128, 128 + TB + GT + NB + E])
        sel = sb("sel", [2 * E, E, 128], F32R)
        zeros = sb("zeros", [128, NT], BF16)
        unused = sb("unused", [128, 3])
        ident = cst[:, 0:128]
        causal = cst[0:TB, 128:128 + TB]
        own = cst[:, 128 + TB:128 + TB + GT]
        row_base = cst[0:TB, 128 + TB + GT:128 + TB + GT + NB]
        expert_no = cst[0:TB, 128 + TB + GT + NB:128 + TB + GT + NB + E]
        top = sb("top", [TB, NB, 8])
        top16 = sb("top16", [TB, NB, KS], F16)
        rep16 = sb("rep16", [TB, GB, H, GT], F16)
        row_idx = sb("row_idx", [TB, NB, KS], I32)
        keyrep = sb("keyrep", [128, GB, NB, KS])
        valid = sb("valid", [128, G, KS])
        vbias = sb("vbias", [128, G, KS])
        mhalf = sb("mhalf", [TB, NB])
        stats = sb("stats", [TB, NB, 6])
        mv = sb("mv", [TB, NB, 2])
        ve = sb("ve", [TB, NB])
        rstd = sb("rstd", [TB, NB])
        xn = sb("xn", [TB, NB, C])
        xnT = sb("xnT", [C, NT])
        on = sb("on", [TB, NB, C])
        xb = sb("xb", [TB, NB, C])
        x1 = sb("x1", [TB, NB, C])
        x2 = xb
        y_out = x1
        aw = sb("aw", [C, H, C])
        mw = sb("mw", [C, H, C])
        simx = sb("simx", [128, 2, CG, KS, GT])
        sim = sb("sim", [128, G, KS])
        s1 = sb("s1", [128, G, KS])
        s2 = sb("s2", [128, G, KS])
        s3 = sb("s3", [128, G, KS])
        ex = sb("ex", [128, G, KS])
        exv = sb("exv", [128, G, KS])
        smax = sb("smax", [128, G])
        ssum = sb("ssum", [128, G])
        srec = sb("srec", [128, G])
        attn = sb("attn", [128, G, KS])
        ltop = sb("ltop", [TB, NB, 8])
        lidx = sb("lidx", [TB, NB, 8], U32)
        lidf = sb("lidf", [TB, NB, 2])
        ld = sb("ld", [TB, NB])
        le = sb("le", [TB, NB])
        lsum = sb("lsum", [TB, NB])
        lw = sb("lw", [TB, NB, 2])
        pick = sb("pick", [TB, NB, 2, E])
        pickw = sb("pickw", [TB, NB, 2, E])
        wi = sb("wi", [TB, NB, E])
        wparts = sb("wparts", [TB, NB, 2, E], F32R)
        wT = sb("wT", [2 * E, NT], F32R)
        yT = sb("yT", [C, NT])
        xnh = sb("xnh", [C, NT], F32R)
        xnl = sb("xnl", [C, NT], F32R)

        with ExitStack() as later:
            sil, gated, hw = (later.enter_context(nc.sbuf_tensor(name, [128, NS, NT], F32))
                              for name in ("sil", "gated", "hw"))
            hh, hl = (later.enter_context(nc.sbuf_tensor(name, [128, NS, NT], F32R)) for name in ("hh", "hl"))
            wb = later.enter_context(nc.sbuf_tensor("wb", [128, 2, NT], F32))
        arena = sb("arena", [128, NB * NV])
        mask_sb = arena[0:TB, :].bitcast(I32).rearrange("p (b v) -> p b v", b=NB)
        attT = arena[0:GR, 0:G * 128].rearrange("p (g r) -> p g r", g=G)
        attx = arena[:, G * 128:G * (128 + GR)].rearrange("p (g k t) -> p g k t", g=G, k=KS)
        cxT = sb("cxT", [C, H, NT])
        vt = (cxT[0:TB, :, :].rearrange("p h n -> p (h n)")[:, 0:NB * KS * C]
              .rearrange("p (b k c) -> p b k c", b=NB, k=KS))
        vgT = sb("vgT", [C, G, KS, GT])
        vg = sb("vg", [GR, G, C])
        qp = sb("qp", [C, G, H, GT])

        with ExitStack() as early:
            def sb_early(name, shape, dt=F32):
                return early.enter_context(nc.sbuf_tensor(name, shape, dt))

            key_w = sb_early("key_w", [TB, NV])
            key = sb_early("key", [TB, 2, NV])
            wx = sb_early("wx", [128, 4, 4, C])
            wa = sb_early("wa", [128, 6, C])
            hid = sb_early("hid", [C, 3, NT])
            x_tok = sb_early("x_tok", [TB, NB, C])
            row = sb_early("row", [TB, 3, C])
            qT = sb_early("qT", [C, NT])
            kT = sb_early("kT", [C, NT])
            v_tok = sb_early("v_tok", [TB, NB, C])
            sT = sb_early("sT", [TB, NB, TB])
        wlo = sb("wlo", [128, WS, 3 * F], F32R)
        whi = sb("whi", [128, WS, 3 * F], F32R)

        x_in = sem("x_in")
        cst_in = sem("cst_in")
        wa_in = sem("wa_in")
        col_in = sem("col_in")
        row_in = sem("row_in")
        mask_in = [sem(f"mask_in{b}") for b in range(NB)]
        wx_in = sem("wx_in")
        gate_in = sem("gate_in")
        raw_in = [sem(f"raw_in{e}") for e in range(E)]
        rows_in = [sem(f"rows_in{b}") for b in range(NB)]
        y_stored = sem("y_stored")
        zeros_ready = sem("zeros_ready")
        sel_ready = sem("sel_ready")
        xb_ready = sem("xb_ready")
        gate_split = sem("gate_split")
        keyw_ready = sem("keyw_ready")
        small_ready = sem("small_ready")
        key_ready = sem("key_ready")
        top_ready = sem("top_ready")
        top16_ready = sem("top16_ready")
        idx_ready = sem("idx_ready")
        keyrep_ps = sem("keyrep_ps")
        keyrep_read = sem("keyrep_read")
        vgT_ps = sem("vgT_ps")
        vgT_ready = sem("vgT_ready")
        vg_ps = sem("vg_ps")
        vg_ready = sem("vg_ready")
        act_small = sem("act_small")
        var_ready = sem("var_ready")
        rstd_ready = sem("rstd_ready")
        xn_ready = sem("xn_ready")
        xnT_ps = sem("xnT_ps")
        xnT_ready = sem("xnT_ready")
        h_ps = sem("h_ps")
        hid_ready = sem("hid_ready")
        qkv_ps = sem("qkv_ps")
        qk_ready = sem("qk_ready")
        v_ready = sem("v_ready")
        s_ps = sem("s_ps")
        sT_ready = sem("sT_ready")
        o_ps = sem("o_ps")
        wh_ps = sem("wh_ps")
        wh_ready = sem("wh_ready")
        qp_ps = sem("qp_ps")
        qp_act = sem("qp_act")
        qp_dve = sem("qp_dve")
        sim_ps = sem("sim_ps")
        sim_read = sem("sim_read")
        sim_summed = sem("sim_summed")
        s3_ready = sem("s3_ready")
        ex_ready = sem("ex_ready")
        attn_ready = sem("attn_ready")
        attx_dve = sem("attx_dve")
        attx_pool = sem("attx_pool")
        attT_ps = sem("attT_ps")
        attT_ready = sem("attT_ready")
        cx_ps = sem("cx_ps")
        cx_act = sem("cx_act")
        cx_dve = sem("cx_dve")
        xo_ps = sem("xo_ps")
        logit_ps = sem("logit_ps")
        ld_ready = sem("ld_ready")
        le_ready = sem("le_ready")
        wparts_ready = sem("wparts_ready")
        wT_ps = sem("wT_ps")
        wT_ready = sem("wT_ready")
        wb_ps = sem("wb_ps")
        wb_ready = sem("wb_ready")
        up_ps = sem("up_ps")
        whi_dve = sem("whi_dve")
        whi_act = sem("whi_act")
        wlo_ready = sem("wlo_ready")
        xnh_ready = sem("xnh_ready")
        xnl_ready = sem("xnl_ready")
        sil_ready = sem("sil_ready")
        gated_ready = sem("gated_ready")
        hw_ready = sem("hw_ready")
        hw_last = sem("hw_last")
        hh_ready = sem("hh_ready")
        hl_ready = sem("hl_ready")
        down_done = sem("down_done")
        yT_ready = sem("yT_ready")
        y_ps = sem("y_ps")
        y_ready = sem("y_ready")
        dve_done = sem("dve_done")

        BX = [bank[0], bank[1], bank[4], bank[5]]
        BG = [bank[6], bank[7], bank[6], bank[7], bank[6], bank[7], bank[7]]
        BS = [bank[0], bank[1], bank[4], bank[5], bank[2]]
        BA = [bank[3], bank[6]]
        BC = [bank[7], bank[0]]
        BO = [bank[1], bank[4], bank[5], bank[2]]
        BT = [bank[1], bank[3], bank[6], bank[7]]
        UP1 = [bank[0], bank[3], bank[6]]
        UP3 = [bank[7], bank[2], bank[5]]
        Y = bank[1]

        def spread_weights(eng, q):
            return eng.tensor_tensor(attx[:, q * QG:(q + 1) * QG, :, :],
                                     attn[:, q * QG:(q + 1) * QG, :].unsqueeze(3)
                                     .broadcast_to([128, QG, KS, GT]),
                                     own.unsqueeze(1).unsqueeze(1).broadcast_to([128, QG, KS, GT]), ALU.mult)

        FILL = [20, 0, 4]
        ROWS_BEFORE = [7, 10]
        SPREAD_BY_POOL = [1, 2, 5, 6]
        SPLIT_BY_ACT = [2, 3, 4]
        CONTEXT_BY_ACT = [0, 1, 2, 5]

        def wait_context(eng, q):
            by_act = sum(p <= q for p in CONTEXT_BY_ACT)
            eng.wait_ge(cx_act, by_act)
            if q + 1 > by_act:
                eng.wait_ge(cx_dve, q + 1 - by_act)

        def context_by_head(copy, q):
            t0, t1 = q * QG * GT, (q + 1) * QG * GT
            return copy(cxT[:, :, t0:t1].rearrange("p h (g t) -> p g h t", t=GT),
                        BC[q % 2][:, :].rearrange("p (g h t) -> p g h t", h=H, t=GT))
        WHOLE = [(0, 3 * F)]
        PARTS = [(p * PW, (p + 1) * PW) for p in range(PIECES)]

        def late_piece(i):
            n = i - 3
            return (EARLY + n // PIECES, n % PIECES) if 0 <= n < (E - EARLY) * PIECES else None

        def lo_count(e):
            return e + 1 if e < EARLY else EARLY + (e - EARLY + 1) * PIECES

        block = stack.enter_context(nc.Block())

        @block.sync
        def _(sp):
            sp.dma_start(x_tok[:, :, :], x.rearrange("(b p) c -> p b c", p=TB)).then_inc(x_in, 16)
            sp.dma_start(mask_sb[:, 0, :], mask[0]).then_inc(mask_in[0], 16)
            sp.dma_start(wa[:, :, :], w_attn).then_inc(wa_in, 16)
            sp.dma_start(mask_sb[:, 1, :], mask[1]).then_inc(mask_in[1], 16)
            sp.dma_start(wx[:, :, :, :], w_x).then_inc(wx_in, 16)
            for b in range(2, NB):
                sp.dma_start(mask_sb[:, b, :], mask[b]).then_inc(mask_in[b], 16)
            sp.dma_start(gate[:, :], w_gate).then_inc(gate_in, 16)
            for e in range(E):
                if e < 2:
                    sp.wait_ge(rows_in[e], 16 * KS)
                if e >= 2:
                    sp.wait_ge(wlo_ready, lo_count(e - 2))
                sp.dma_start(raw[:, e % 2, :], w_ffn[e]).then_inc(raw_in[e], 16)
            for n in range(2):
                sp.wait_ge(y_ready, n + 1)
                sp.dma_start(out.rearrange("(b p) c -> p b c", p=TB)[:, 2 * n:2 * n + 2, :],
                             y_out[:, 2 * n:2 * n + 2, :]).then_inc(y_stored, 16)
            sp.wait_ge(y_stored, 32)

        @block.gpsimd
        def _(pool):
            pool.memset(mhalf[:, :], -0.5).then_inc(small_ready, 1)
            pool.iota(key_w[:, :], [[-1, NV]], base=NV, channel_multiplier=0,
                      allow_small_or_imprecise_dtypes=True).then_inc(keyw_ready, 1)

            def rsqrt(n, b0=0, b1=NB):
                if n == 0:
                    pool.wait_ge(small_ready, 1)
                pool.wait_ge(var_ready, n + 1)
                pool.tensor_tensor(rstd[:, b0:b1], ve[:, b0:b1], mhalf[:, b0:b1],
                                   ALU.pow).then_inc(rstd_ready, 1)

            def gather(j0, j1):
                for j in range(j0, j1):
                    b, k = j // KS, j % KS
                    if j == j0 or k == 0:
                        pool.wait_ge(idx_ready, b + 1)
                    pool.indirect_dma_start(
                        out=vt[:, b, k, :], out_offset=None, in_=ctx_rows,
                        in_offset=bass.IndirectOffsetOnAxis(ap=row_idx[:, b, k:k + 1], axis=0),
                    ).then_inc(rows_in[b], 16)

            rsqrt(0)
            pool.wait_ge(x_in, 16)
            pool.wait_ge(row_in, 16)
            pool.tensor_tensor(xb[:, :, :], x_tok[:, :, :], row[:, 2, :].unsqueeze(1).broadcast_to([TB, NB, C]),
                               ALU.add).then_inc(xb_ready, 1)
            pool.wait_ge(cst_in, 16)
            pool.tensor_tensor(sel[:, :, :], ident[0:2 * E, 0:E].unsqueeze(2).broadcast_to([2 * E, E, 128]),
                               ident[0:2 * E, E:2 * E].unsqueeze(2).broadcast_to([2 * E, E, 128]),
                               ALU.add).then_inc(sel_ready, 1)
            gather(0, ROWS_BEFORE[0])
            rsqrt(1)
            gather(ROWS_BEFORE[0], ROWS_BEFORE[1])
            rsqrt(2)
            gather(ROWS_BEFORE[1], NB * KS)

            def split_low(e, p, a, z):
                if e in SPLIT_BY_ACT:
                    pool.wait_ge(whi_act, SPLIT_BY_ACT.index(e) + 1)
                else:
                    pool.wait_ge(whi_dve, e + 1 if e < EARLY else EARLY - len(SPLIT_BY_ACT) + (e - EARLY) * PIECES + p + 1)
                pool.tensor_tensor(wlo[:, e % WS, a:z], raw[:, e % 2, a:z],
                                   whi[:, e % WS, a:z].bitcast(F32), ALU.subtract).then_inc(wlo_ready, 1)

            split_low(0, 0, *WHOLE[0])
            for q in SPREAD_BY_POOL[0:2]:
                pool.wait_ge(attn_ready, 1)
                spread_weights(pool, q).then_inc(attx_pool, 1)
            split_low(1, 0, *WHOLE[0])
            for q in SPREAD_BY_POOL[2:4]:
                pool.wait_ge(attn_ready, 2)
                spread_weights(pool, q).then_inc(attx_pool, 1)
            split_low(2, 0, *WHOLE[0])
            rsqrt(3, 0, 1)
            split_low(3, 0, *WHOLE[0])
            for b in range(1, NB):
                rsqrt(3 + b, b, b + 1)
            split_low(4, 0, *WHOLE[0])
            for i in range(NCH - 1):
                e = i // FC
                pool.wait_ge(wb_ready, e + 1)
                if i >= NS:
                    pool.wait_ge(hl_ready, i - NS + 1)
                pool.wait_ge(gated_ready, i + 1)
                pool.tensor_tensor(hw[:, i % NS, :], gated[:, i % NS, :], wb[:, e % 2, :],
                                   ALU.mult).then_inc(hw_ready, 1)
                if late_piece(i):
                    split_low(*late_piece(i), *PARTS[late_piece(i)[1]])

        @block.scalar
        def _(act):
            act.dma_start(cst[:, :], consts).then_inc(cst_in, 16)
            act.dma_start(col[:, :], cols).then_inc(col_in, 16)
            act.dma_start(row[:, :, :], rows.partition_broadcast(TB)).then_inc(row_in, 16)
            act.wait_ge(zeros_ready, 1)
            act.activation(unused[:, 0:1], zeros[:, 0:1], ACT.Gelu)
            act.wait_ge(cst_in, 16)
            act.copy(rep16[:, :, :, :], ident[0:TB, 0:TB].rearrange("p (i t) -> p i t", t=GT).unsqueeze(2)
                     .broadcast_to([TB, GB, H, GT])).then_inc(act_small, 1)
            act.wait_ge(col_in, 16)
            act.wait_ge(xnT_ps, 1)
            act.copy(xnT[:, :], bank[0][:, 0:NT]).then_inc(xnT_ready, 1)
            for n in range(3):
                act.wait_ge(h_ps, n + 1)
                act.activation(hid[:, n, :], bank[1 + n][:, 0:NT], ACT.Gelu,
                               bias=col[:, n:n + 1]).then_inc(hid_ready, 1)
            for n, dst in enumerate([qT, kT]):
                act.wait_ge(qkv_ps, n + 1)
                act.activation(dst[:, :], bank[4 + n][:, 0:NT], ACT.Identity,
                               bias=col[:, 3 + n:4 + n]).then_inc(qk_ready, 1)
            for n in range(4):
                act.wait_ge(wh_ps, n + 1)
                act.mul((aw if n < 2 else mw)[:, n % 2:H:2, :],
                        bank[4 + n % 2][:, :].rearrange("p (j c) -> p j c", c=C),
                        DH ** -0.5 if n < 2 else 1.0).then_inc(wh_ready, 1)

            def rows_channels_first(b):
                for i, (k0, k1) in enumerate([(0, 4), (4, KS)]):
                    act.wait_ge(vgT_ps, 2 * b + i + 1)
                    act.copy(vgT[:, b * GB:(b + 1) * GB, k0:k1, :].rearrange("p g k t -> p k g t"),
                             bank[2 + i][:, 0:(k1 - k0) * TB].rearrange("p (k g t) -> p k g t", g=GB, t=GT)
                             ).then_inc(vgT_ready, 1)

            def rows_by_group(q):
                act.wait_ge(vg_ps, q + 1)
                act.copy(vg[:, q * QG:(q + 1) * QG, :].rearrange("p g c -> p (g c)"),
                         BG[q][0:GR, :]).then_inc(vg_ready, 1)

            rows_channels_first(0)
            rows_by_group(0)
            act.wait_ge(xnT_ps, 2)
            act.activation(xnT[:, :], bank[0][:, 0:NT], ACT.Identity, bias=col[:, 6:7],
                           scale=col[:, 5:6]).then_inc(xnT_ready, 1)
            rows_channels_first(1)
            for h in range(0, H, 2):
                act.wait_ge(qp_ps, h + 1)
                act.copy(qp[:, :, h, :], BX[h % 4][:, 0:NT].rearrange("p (g t) -> p g t", t=GT)
                         ).then_inc(qp_act, 1)
                if h < 4:
                    rows_by_group(h // 2 + 1)
            rows_channels_first(2)
            act.activation(unused[:, 1:2], zeros[:, 0:1], ACT.Exp)
            rows_channels_first(3)
            rows_by_group(3)

            def exponentials(n):
                g0, g1 = CHUNKS[HALVES[n][0]][0], CHUNKS[HALVES[n][1] - 1][1]
                act.wait_ge(s3_ready, n + 1)
                act.activation(ex[:, g0:g1, :], s3[:, g0:g1, :], ACT.Exp).then_inc(ex_ready, 1)

            def weights_by_row(q):
                act.wait_ge(attT_ps, q + 1)
                act.copy(attT[:, q * QG:(q + 1) * QG, :].rearrange("p g r -> p (g r)"),
                         BA[q % 2][0:GR, :]).then_inc(attT_ready, 1)

            def context(q):
                act.wait_ge(cx_ps, q + 1)
                context_by_head(act.copy, q).then_inc(cx_act, 1)

            def split_high(e):
                act.wait_ge(raw_in[e], 16)
                act.copy(whi[:, e % WS, :], raw[:, e % 2, :]).then_inc(whi_act, 1)

            def tokens_high(b):
                act.wait_ge(xnT_ps, 3 + b)
                act.copy(xnh[:, b * TB:(b + 1) * TB], BT[b][:, 0:TB]).then_inc(xnh_ready, 1)

            exponentials(0)
            rows_by_group(4)
            weights_by_row(0)
            rows_by_group(5)
            weights_by_row(1)
            weights_by_row(2)
            context(0)
            context(1)
            exponentials(1)
            context(2)
            split_high(2)
            weights_by_row(3)
            weights_by_row(4)
            rows_by_group(6)
            weights_by_row(5)
            split_high(3)
            tokens_high(0)
            weights_by_row(6)
            context(5)
            tokens_high(1)
            split_high(4)
            tokens_high(2)
            tokens_high(3)
            act.wait_ge(ld_ready, 1)
            act.activation(le[:, :], ld[:, :], ACT.Exp).then_inc(le_ready, 1)

            def weight_copy(e):
                act.wait_ge(wb_ps, e + 1)
                if e >= 2:
                    act.wait_ge(hw_ready, FC * (e - 1))
                act.copy(wb[:, e % 2, :], bank[4][:, 0:NT]).then_inc(wb_ready, 1)

            def silu(i):
                if i >= NS:
                    act.wait_ge(gated_ready, i - NS + 1)
                act.wait_ge(up_ps, 2 * i + 1)
                act.activation(sil[:, i % NS, :], UP1[i % 3][:, 0:NT], ACT.Silu).then_inc(sil_ready, 1)

            def hidden_high(i):
                if i >= NS:
                    act.wait_ge(down_done, i - NS + 1)
                if i < NCH - 1:
                    act.wait_ge(hw_ready, i + 1)
                else:
                    act.wait_ge(hw_last, 1)
                act.copy(hh[:, i % NS, :], hw[:, i % NS, :]).then_inc(hh_ready, 1)

            silu(0)
            silu(1)
            weight_copy(0)
            silu(2)
            hidden_high(0)
            for i in range(3, NCH + 2):
                hidden_high(i - 2)
                if i < NCH:
                    silu(i)
                    if i % FC == 3 and i // FC + 1 < E:
                        weight_copy(i // FC + 1)

        @block.vector
        def _(dve):
            chain = [0]

            def then(ins):
                chain[0] += 1
                ins.then_inc(dve_done, 1)
                dve.wait_ge(dve_done, chain[0])

            def mark_rows(b):
                if b == 0:
                    dve.wait_ge(keyw_ready, 1)
                dve.wait_ge(mask_in[b], 16)
                dve.scalar_tensor_tensor(out=key[:, b % 2, :], in0=mask_sb[:, b, :], scalar=0.0,
                                         in1=key_w[:, :], op0=ALU.not_equal,
                                         op1=ALU.mult).then_inc(key_ready, 1)

            def index_rows(b):
                dve.wait_ge(key_ready, b + 1)
                dve.max(top[:, b, :], key[:, b % 2, :]).then_inc(top_ready, 1)
                dve.wait_ge(top_ready, b + 1)
                dve.scalar_tensor_tensor(out=row_idx[:, b, :], in0=top[:, b, 0:KS], scalar=1.0,
                                         in1=row_base[:, b:b + 1].broadcast_to([TB, KS]), op0=ALU.max,
                                         op1=ALU.subtract, reverse1=True).then_inc(idx_ready, 1)

            def variance(src, b0=0, b1=NB):
                for b in range(b0, b1):
                    last = dve.bn_stats(stats[:, b, :], src[:, b, :])
                then(last)
                for b in range(b0, b1):
                    last = dve.bn_aggr(mv[:, b, :], stats[:, b, :])
                then(last)

            def variance_eps(b0=0, b1=NB, scale=1.0, eps=EPS):
                dve.tensor_scalar(ve[:, b0:b1], mv[:, b0:b1, 1], scale, eps, ALU.mult,
                                  ALU.add).then_inc(var_ready, 1)

            def normalise(dst, src, b0=0, b1=NB):
                for b in range(b0, b1):
                    last = dve.tensor_scalar(dst[:, b, :], src[:, b, :], mv[:, b, 0:1], rstd[:, b:b + 1],
                                             ALU.subtract, ALU.mult)
                return last

            def blocks(ap, n):
                return ap.unsqueeze(1).broadcast_to([ap.shape[0], n, ap.shape[1]])

            dve.memset(zeros[:, :], 0.0).then_inc(zeros_ready, 1)
            dve.wait_ge(x_in, 16)
            variance(x_tok)
            dve.wait_ge(cst_in, 16)
            variance_eps()
            dve.wait_ge(rstd_ready, 1)
            normalise(xn, x_tok).then_inc(xn_ready, 1)
            mark_rows(0)
            index_rows(0)
            mark_rows(1)
            index_rows(1)
            dve.wait_ge(row_in, 16)
            dve.wait_ge(qkv_ps, 3)
            dve.tensor_tensor(v_tok[:, :, :], bank[6][0:TB, :].rearrange("p (b c) -> p b c", b=NB),
                              blocks(row[:, 0, :], NB), ALU.add).then_inc(v_ready, 1)
            dve.wait_ge(s_ps, 1)
            dve.tensor_tensor(sT[:, :, :], bank[0][0:TB, 0:NB * TB].rearrange("p (b c) -> p b c", b=NB),
                              blocks(causal, NB), ALU.mult).then_inc(sT_ready, 1)
            dve.wait_ge(o_ps, 1)
            o_tok = bank[1][0:TB, :].rearrange("p (b c) -> p b c", b=NB)
            variance(o_tok)
            variance_eps()
            for b in range(NB):
                last = dve.scalar_tensor_tensor(out=on[:, b, :], in0=o_tok[:, b, :], scalar=mv[:, b, 0:1],
                                                in1=row[:, 1, :], op0=ALU.subtract, op1=ALU.mult)
            then(last)
            dve.wait_ge(xb_ready, 1)
            dve.wait_ge(rstd_ready, 2)
            for b in range(NB):
                last = dve.scalar_tensor_tensor(out=x1[:, b, :], in0=on[:, b, :], scalar=rstd[:, b:b + 1],
                                                in1=xb[:, b, :], op0=ALU.mult, op1=ALU.add)
            then(last)
            variance(x1)
            variance_eps(scale=1.0 + EPS, eps=EPS * EPS)
            mark_rows(2)
            dve.wait_ge(rstd_ready, 3)
            normalise(xn, x1).then_inc(xn_ready, 1)
            index_rows(2)
            mark_rows(3)
            index_rows(3)
            dve.tensor_copy(top16[:, :, :], top[:, :, 0:KS]).then_inc(top16_ready, 1)
            def split_high(e, a, z):
                dve.wait_ge(raw_in[e], 16)
                if e >= WS:
                    dve.wait_ge(down_done, FC * (e - WS + 1))
                dve.tensor_copy(whi[:, e % WS, a:z], raw[:, e % 2, a:z]).then_inc(whi_dve, 1)

            dve.wait_ge(gate_in, 16)
            dve.tensor_copy(gate_hi[:, :], gate[:, :]).then_inc(gate_split, 1)
            dve.wait_ge(gate_split, 1)
            dve.tensor_tensor(gate_lo[:, :], gate[:, :], gate_hi[:, :].bitcast(F32),
                              ALU.subtract).then_inc(gate_split, 1)
            for h in range(1, H, 2):
                dve.wait_ge(qp_ps, h + 1)
                dve.tensor_copy(qp[:, :, h, :], BX[h % 4][:, 0:NT].rearrange("p (g t) -> p g t", t=GT)
                                ).then_inc(qp_dve, 1)
                if h == 3:
                    dve.wait_ge(keyrep_ps, 1)
                    dve.tensor_copy(keyrep[:, :, :, :].rearrange("p i b k -> p (i b k)"),
                                    bank[6][:, 0:GB * NB * KS]).then_inc(keyrep_read, 1)
                    dve.wait_ge(keyrep_read, 1)
                    then(dve.tensor_scalar(valid[:, :, :].rearrange("p (b i) k -> p b i k", b=NB),
                                           keyrep[:, :, :, :].rearrange("p i b k -> p b i k"), 1.0, None, ALU.min))
                    dve.tensor_scalar(vbias[:, :, :], valid[:, :, :], 10000.0, -10000.0, ALU.mult, ALU.add)
            split_high(0, *WHOLE[0])
            split_high(1, *WHOLE[0])

            def own_scores(c0, c1):
                for c in range(c0, c1 + 1):
                    if c < c1:
                        a, z = CHUNKS[c]
                        dve.wait_ge(sim_ps, c + 1)
                        if c >= 2:
                            dve.wait_ge(sim_summed, c - 1)
                        dve.tensor_tensor(simx[:, c % 2, 0:z - a, :, :],
                                          BS[c][:, 0:(z - a) * GR].rearrange("p (g k t) -> p g k t", t=GT, k=KS),
                                          own.unsqueeze(1).unsqueeze(1).broadcast_to([128, z - a, KS, GT]),
                                          ALU.mult).then_inc(sim_read, 1)
                    if c > c0:
                        a, z = CHUNKS[c - 1]
                        dve.wait_ge(sim_read, c)
                        dve.tensor_reduce(sim[:, a:z, :], simx[:, (c - 1) % 2, 0:z - a, :, :],
                                          AX.X, ALU.add).then_inc(sim_summed, 1)
                dve.wait_ge(sim_summed, c1)

            def softmax(n):
                g0, g1 = CHUNKS[HALVES[n][0]][0], CHUNKS[HALVES[n][1] - 1][1]
                g = slice(g0, g1)

                def over_rows(ap):
                    return ap[:, g].unsqueeze(2).broadcast_to([128, g1 - g0, KS])

                then(dve.tensor_tensor(s1[:, g, :], sim[:, g, :], valid[:, g, :], ALU.mult))
                then(dve.tensor_tensor(s2[:, g, :], s1[:, g, :], vbias[:, g, :], ALU.add))
                then(dve.tensor_reduce(smax[:, g], s2[:, g, :], AX.X, ALU.max))
                dve.tensor_tensor(s3[:, g, :], s2[:, g, :], over_rows(smax), ALU.subtract
                                  ).then_inc(s3_ready, 1)
                dve.wait_ge(ex_ready, n + 1)
                then(dve.tensor_reduce(ssum[:, g], ex[:, g, :], AX.X, ALU.add))
                dve.reciprocal(srec[:, g], ssum[:, g])
                then(dve.tensor_tensor(exv[:, g, :], ex[:, g, :], valid[:, g, :], ALU.mult))
                dve.tensor_tensor(attn[:, g, :], exv[:, g, :], over_rows(srec), ALU.mult
                                  ).then_inc(attn_ready, 1)
                dve.wait_ge(attn_ready, n + 1)
                for q in range(g0 // QG, g1 // QG):
                    if q not in SPREAD_BY_POOL:
                        spread_weights(dve, q).then_inc(attx_dve, 1)

            for n, (c0, c1) in enumerate(HALVES):
                own_scores(c0, c1)
                softmax(n)

            def context(q):
                dve.wait_ge(cx_ps, q + 1)
                context_by_head(dve.tensor_copy, q).then_inc(cx_dve, 1)

            def add_context(b):
                dve.wait_ge(xo_ps, b + 1)
                then(dve.tensor_tensor(x2[:, b, :], x1[:, b, :], BO[b][0:TB, 0:C], ALU.add))
                variance(x2, b, b + 1)
                variance_eps(b, b + 1)

            def norm_context(b):
                dve.wait_ge(rstd_ready, 4 + b)
                normalise(xn, x2, b, b + 1).then_inc(xn_ready, 1)

            def tokens_low(b):
                t = slice(b * TB, (b + 1) * TB)
                dve.wait_ge(xnh_ready, b + 1)
                dve.tensor_tensor(xnl[:, t], BT[b][:, 0:TB], xnh[:, t].bitcast(F32),
                                  ALU.subtract).then_inc(xnl_ready, 1)

            context(3)
            add_context(0)
            context(4)
            norm_context(0)
            add_context(1)
            context(6)
            norm_context(1)
            tokens_low(0)
            add_context(2)
            norm_context(2)
            tokens_low(1)
            add_context(3)
            norm_context(3)
            tokens_low(2)
            tokens_low(3)

            def gate_hidden(i):
                if i >= NS:
                    dve.wait_ge(hw_ready, i - NS + 1)
                dve.wait_ge(up_ps, 2 * i + 2)
                dve.wait_ge(sil_ready, i + 1)
                dve.tensor_tensor(gated[:, i % NS, :], sil[:, i % NS, :], UP3[i % 3][:, 0:NT],
                                  ALU.mult).then_inc(gated_ready, 1)

            dve.wait_ge(logit_ps, NB)
            logits = bank[4][0:TB, 0:NB * E].rearrange("p (b e) -> p b e", b=NB)
            for b in range(NB):
                last = dve.max(ltop[:, b, :], logits[:, b, :])
            then(last)
            dve.tensor_tensor(ld[:, :], ltop[:, :, 1], ltop[:, :, 0], ALU.subtract).then_inc(ld_ready, 1)
            for b in range(NB):
                last = dve.max_index(lidx[:, b, :], ltop[:, b, :], logits[:, b, :])
            then(last)
            then(dve.tensor_copy(lidf[:, :, :], lidx[:, :, 0:2]))
            dve.tensor_tensor(pick[:, :, :, :],
                              expert_no.unsqueeze(1).unsqueeze(1).broadcast_to([TB, NB, 2, E]),
                              lidf[:, :, :].unsqueeze(3).broadcast_to([TB, NB, 2, E]), ALU.is_equal)
            dve.wait_ge(le_ready, 1)
            then(dve.tensor_scalar(lsum[:, :], le[:, :], 1.0, None, ALU.add))
            then(dve.reciprocal(lw[:, :, 0], lsum[:, :]))
            then(dve.tensor_tensor(lw[:, :, 1], le[:, :], lw[:, :, 0], ALU.mult))
            then(dve.tensor_tensor(pickw[:, :, :, :], pick[:, :, :, :],
                                   lw[:, :, :].unsqueeze(3).broadcast_to([TB, NB, 2, E]), ALU.mult))
            then(dve.tensor_tensor(wi[:, :, :], pickw[:, :, 0, :], pickw[:, :, 1, :], ALU.add))
            then(dve.tensor_copy(wparts[:, :, 0, :], wi[:, :, :]))
            dve.tensor_tensor(wparts[:, :, 1, :], wi[:, :, :], wparts[:, :, 0, :].bitcast(F32),
                              ALU.subtract).then_inc(wparts_ready, 1)
            dve.wait_ge(wT_ps, 1)
            dve.tensor_copy(wT[:, :], bank[4][0:2 * E, 0:NT]).then_inc(wT_ready, 1)
            gate_hidden(0)
            gate_hidden(1)
            for i in range(2, NCH + 2):
                if i < NCH:
                    gate_hidden(i)
                dve.wait_ge(hh_ready, i - 1)
                dve.tensor_tensor(hl[:, (i - 2) % NS, :], hw[:, (i - 2) % NS, :],
                                  hh[:, (i - 2) % NS, :].bitcast(F32), ALU.subtract).then_inc(hl_ready, 1)
                if i == NCH - 1:
                    dve.wait_ge(gated_ready, NCH)
                    dve.tensor_tensor(hw[:, i % NS, :], gated[:, i % NS, :], wb[:, (E - 1) % 2, :],
                                      ALU.mult).then_inc(hw_last, 1)
                if late_piece(i):
                    split_high(late_piece(i)[0], *PARTS[late_piece(i)[1]])
            dve.wait_ge(down_done, NCH)
            for n in range(2):
                t = slice(n * NT // 2, (n + 1) * NT // 2)
                dve.tensor_copy(yT[:, t], Y[:, t]).then_inc(yT_ready, 1)
            for n in range(2):
                b = slice(2 * n, 2 * n + 2)
                dve.wait_ge(y_ps, n + 1)
                dve.tensor_tensor(y_out[:, b, :], x2[:, b, :],
                                  bank[4 + n][0:TB, 0:2 * C].rearrange("p (b c) -> p b c", b=2),
                                  ALU.add).then_inc(y_ready, 1)

        @block.tensor
        def _(pe):
            def turn_tokens(n):
                pe.wait_ge(xn_ready, n + 1)
                for b in range(NB):
                    last = pe.transpose(bank[0][:, b * TB:(b + 1) * TB], xn[:, b, :], ident[0:TB, 0:TB])
                last.then_inc(xnT_ps, 1)

            def keep_warm(b, n):
                for _ in range(n):
                    pe.matmul(bank[b][:, 0:NT], zeros[:, 0:128], zeros[:, :], start=True, stop=True)

            pe.wait_ge(zeros_ready, 1)
            keep_warm(7, 17)
            pe.wait_ge(cst_in, 16)
            turn_tokens(0)
            pe.wait_ge(wa_in, 16)
            pe.wait_ge(xnT_ready, 1)
            for n in range(3):
                pe.matmul(bank[1 + n][:, 0:NT], wa[:, n, :], xnT[:, :], start=True, stop=True).then_inc(h_ps, 1)
            for n in range(2):
                pe.wait_ge(hid_ready, n + 1)
                pe.matmul(bank[4 + n][:, 0:NT], wa[:, 3 + n, :], hid[:, n, :],
                          start=True, stop=True).then_inc(qkv_ps, 1)
            pe.wait_ge(hid_ready, 3)
            for b in range(NB):
                last = pe.matmul(bank[6][0:TB, b * C:(b + 1) * C], hid[:, 2, b * TB:(b + 1) * TB],
                                 wa[:, 5, :], start=True, stop=True)
            last.then_inc(qkv_ps, 1)
            pe.wait_ge(qk_ready, 2)
            for b in range(NB):
                t = slice(b * TB, (b + 1) * TB)
                last = pe.matmul(bank[0][0:TB, t], kT[:, t], qT[:, t], start=True, stop=True)
            last.then_inc(s_ps, 1)
            pe.wait_ge(wx_in, 16)

            def head_weights(n):
                if n >= 2:
                    pe.wait_ge(wh_ready, n - 1)
                p = slice(DH * (n % 2), DH * (n % 2) + DH)
                for j in range(4):
                    last = pe.matmul(bank[4 + n % 2][:, j * C:(j + 1) * C],
                                     wx[p, 2 * (n // 2), j, :], wx[p, 2 * (n // 2) + 1, j, :],
                                     start=True, stop=True)
                last.then_inc(wh_ps, 1)

            head_weights(0)
            pe.wait_ge(v_ready, 1)
            pe.wait_ge(sT_ready, 1)
            for b in range(NB):
                last = pe.matmul(bank[1][0:TB, b * C:(b + 1) * C], sT[:, b, :], v_tok[:, b, :],
                                 start=True, stop=True)
            last.then_inc(o_ps, 1)
            for n in range(1, 4):
                head_weights(n)

            def rows_channels_first(b):
                pe.wait_ge(rows_in[b], 16 * KS)
                for i, (k0, k1) in enumerate([(0, 4), (4, KS)]):
                    if b >= 1:
                        pe.wait_ge(vgT_ready, 2 * (b - 1) + i + 1)
                    for k in range(k0, k1):
                        last = pe.transpose(bank[2 + i][:, (k - k0) * TB:(k - k0 + 1) * TB], vt[:, b, k, :],
                                            ident[0:TB, 0:TB])
                    last.then_inc(vgT_ps, 1)

            def rows_by_group(q):
                pe.wait_ge(vgT_ready, 2 * (((q + 1) * QG - 1) // GB + 1))
                if q == QUADS - 1:
                    wait_context(pe, 2)
                elif q >= 2:
                    pe.wait_ge(vg_ready, q - 1)
                for j in range(QG):
                    last = pe.transpose(BG[q][0:GR, j * C:(j + 1) * C],
                                        vgT[:, q * QG + j, :, :].rearrange("p k t -> p (k t)"), ident)
                last.then_inc(vg_ps, 1)

            rows_channels_first(0)
            rows_by_group(0)
            keep_warm(7, FILL[0])
            turn_tokens(1)
            rows_channels_first(1)
            pe.wait_ge(wh_ready, 4)
            pe.wait_ge(xnT_ready, 2)
            for h in range(H):
                if h >= 4:
                    pe.wait_ge(qp_dve if h % 2 else qp_act, (h - 4) // 2 + 1)
                pe.matmul(BX[h % 4][:, 0:NT], aw[:, h, :], xnT[:, :], start=True, stop=True).then_inc(qp_ps, 1)
                if h in (1, 3):
                    rows_by_group((h + 1) // 2)
                if h == 5:
                    pe.wait_ge(act_small, 1)
                    pe.wait_ge(top16_ready, 1)
                    pe.wait_ge(vg_ready, 3)
                    for i in range(GB):
                        last = pe.matmul(bank[6][:, i * NB * KS:(i + 1) * NB * KS],
                                         rep16[:, i, :, :].rearrange("p h t -> p (h t)"),
                                         top16[:, :, :], start=True, stop=True)
                    last.then_inc(keyrep_ps, 1)
            rows_channels_first(2)
            pe.wait_ge(qp_act, H // 2)
            pe.wait_ge(qp_dve, H // 2)
            for c, (a, z) in enumerate(CHUNKS):
                b = (z - 1) // GB
                if b == NB - 1 and (a - 1) // GB < b:
                    pe.wait_ge(keyrep_read, 1)
                    rows_channels_first(b)
                    rows_by_group(3)
                    rows_by_group(4)
                pe.wait_ge(vgT_ready, 2 * (b + 1))
                for g in range(a, z):
                    last = pe.matmul(BS[c][:, (g - a) * GR:(g - a + 1) * GR],
                                     qp[:, g, :, :].rearrange("p h t -> p (h t)"),
                                     vgT[:, g, :, :].rearrange("p k t -> p (k t)"), start=True, stop=True)
                last.then_inc(sim_ps, 1)

            def weights_by_row(q):
                if q in SPREAD_BY_POOL:
                    pe.wait_ge(attx_pool, SPREAD_BY_POOL.index(q) + 1)
                else:
                    pe.wait_ge(attx_dve, q + 1 - sum(p < q for p in SPREAD_BY_POOL))
                if q >= 2:
                    pe.wait_ge(attT_ready, q - 1)
                for j in range(QG):
                    last = pe.transpose(BA[q % 2][0:GR, j * 128:(j + 1) * 128],
                                        attx[:, q * QG + j, :, :].rearrange("p k t -> p (k t)"), ident)
                last.then_inc(attT_ps, 1)

            def context(q):
                pe.wait_ge(attT_ready, q + 1)
                if q >= 2:
                    wait_context(pe, q - 2)
                for j in range(QG):
                    g = q * QG + j
                    last = pe.matmul(BC[q % 2][:, j * 128:(j + 1) * 128], vg[:, g, :], attT[:, g, :],
                                     start=True, stop=True)
                last.then_inc(cx_ps, 1)

            def output(b):
                wait_context(pe, ((b + 1) * GB - 1) // QG)
                for h in range(H):
                    last = pe.matmul(BO[b][0:TB, 0:C], cxT[:, h, b * TB:(b + 1) * TB],
                                     mw[:, h, :], start=(h == 0), stop=(h == H - 1))
                last.then_inc(xo_ps, 1)

            def turn_block(b):
                pe.wait_ge(xn_ready, 3 + b)
                pe.transpose(BT[b][:, 0:TB], xn[:, b, :], ident[0:TB, 0:TB]).then_inc(xnT_ps, 1)

            def logits(b):
                pe.wait_ge(gate_split, 2)
                pe.wait_ge(xnl_ready, b + 1)
                t = slice(b * TB, (b + 1) * TB)
                part = bank[4][0:TB, b * E:(b + 1) * E]
                pe.matmul(part, xnh[:, t], gate_hi[:, :], start=True, stop=False)
                pe.matmul(part, xnh[:, t], gate_lo[:, :], start=False, stop=False)
                pe.matmul(part, xnl[:, t], gate_hi[:, :], start=False, stop=True).then_inc(logit_ps, 1)

            weights_by_row(0)
            rows_by_group(5)
            pe.wait_ge(vg_ready, 5)
            weights_by_row(1)
            weights_by_row(2)
            pe.wait_ge(vg_ready, 6)
            context(0)
            context(1)
            context(2)
            output(0)
            weights_by_row(3)
            weights_by_row(4)
            rows_by_group(6)
            context(3)
            weights_by_row(5)
            pe.wait_ge(vg_ready, QUADS)
            context(4)
            output(1)
            turn_block(0)
            weights_by_row(6)
            context(5)
            context(6)
            output(2)
            turn_block(1)
            logits(0)
            output(3)
            keep_warm(0, FILL[1])
            turn_block(2)
            logits(1)
            keep_warm(0, FILL[2])
            turn_block(3)
            logits(2)
            logits(3)

            def product(out, part, e, c, high, low, start, stop):
                w = slice(part * F + c * 128, part * F + (c + 1) * 128)
                pe.matmul(out, whi[:, e % WS, w], high, start=start, stop=False, skip_group_check=True)
                pe.matmul(out, wlo[:, e % WS, w], high, start=False, stop=False, skip_group_check=True)
                return pe.matmul(out, whi[:, e % WS, w], low, start=False, stop=stop, skip_group_check=True)

            def up_w1(i):
                if i % FC == 0:
                    pe.wait_ge(wlo_ready, lo_count(i // FC))
                if i >= 3:
                    pe.wait_ge(sil_ready, i - 2)
                product(UP1[i % 3][:, 0:NT], 0, i // FC, i % FC, xnh[:, :], xnl[:, :],
                        True, True).then_inc(up_ps, 1)

            def up_w3(i):
                if i >= 3:
                    pe.wait_ge(gated_ready, i - 2)
                product(UP3[i % 3][:, 0:NT], 1, i // FC, i % FC, xnh[:, :], xnl[:, :],
                        True, True).then_inc(up_ps, 1)

            def down(i):
                pe.wait_ge(hl_ready, i + 1)
                product(Y[:, 0:NT], 2, i // FC, i % FC, hh[:, i % NS, :], hl[:, i % NS, :],
                        i == 0, i == NCH - 1).then_inc(down_done, 1)

            def weights_of(e):
                if e >= 1:
                    pe.wait_ge(wb_ready, e)
                pe.matmul(bank[4][:, 0:NT], sel[:, e, :], wT[:, :], start=True, stop=True).then_inc(wb_ps, 1)

            for i in range(2):
                up_w1(i)
                up_w3(i)
            up_w1(2)
            pe.wait_ge(wparts_ready, 1)
            for b in range(NB):
                last = pe.transpose(bank[4][0:2 * E, b * TB:(b + 1) * TB],
                                    wparts[:, b, :, :].rearrange("p a e -> p (a e)").bitcast(F32),
                                    ident[0:TB, 0:TB])
            last.then_inc(wT_ps, 1)
            pe.wait_ge(wT_ready, 1)
            pe.wait_ge(sel_ready, 1)
            weights_of(0)
            up_w3(2)
            for i in range(3, NCH + LAG):
                if i < NCH:
                    up_w1(i)
                    up_w3(i)
                    if i % FC == 3 and i // FC + 1 < E:
                        weights_of(i // FC + 1)
                if i >= LAG:
                    down(i - LAG)
            for n in range(2):
                pe.wait_ge(yT_ready, n + 1)
                for i in range(2):
                    b = 2 * n + i
                    last = pe.transpose(bank[4 + n][0:TB, i * C:(i + 1) * C], yT[:, b * TB:(b + 1) * TB], ident)
                last.then_inc(y_ps, 1)


def kernel(x, ctx_1024, mask_BxS2xS_ik0, L0_attn_W1q, L0_attn_b1q, L0_attn_W2q, L0_attn_b2q, L0_attn_W1k,
           L0_attn_b1k, L0_attn_W2k, L0_attn_b2k, L0_attn_W1v, L0_attn_b1v, L0_attn_W2v, L0_attn_b2v,
           L0_attn_ln_w, L0_attn_ln_b, L0_xattn_ln_w, L0_xattn_ln_b, L0_xattn_Wq, L0_xattn_Wkv,
           L0_xattn_Wout, L0_ffn_gate_w, L0_ffn_w1, L0_ffn_w3, L0_ffn_w2):
    import numpy as np
    import concourse.bacc as bacc
    from concourse.bass_utils import run_bass_kernel_spmd

    a = np.asarray
    INNER = H * DH

    def by_heads(w):
        return a(w).reshape(H // 2, 2 * DH, C).transpose(1, 0, 2)

    wkv = a(L0_xattn_Wkv)
    consts = np.zeros((128, 128 + TB + GT + NB + E), np.float32)
    consts[:, 0:128] = np.eye(128)
    j, i = np.arange(TB)[:, None], np.arange(TB)[None, :]
    consts[0:TB, 128:128 + TB] = ((j <= i) & (j // SEQ == i // SEQ)) / np.float32(SCORE_SCALE)
    consts[:, 128 + TB:128 + TB + GT] = np.arange(128)[:, None] % GT == np.arange(GT)[None, :]
    batch = (np.arange(NB)[None, :] * TB + np.arange(TB)[:, None]) // SEQ
    consts[0:TB, 128 + TB + GT:128 + TB + GT + NB] = NV * (batch + 1)
    consts[:, 128 + TB + GT + NB:] = np.arange(E)

    arrays = {
        "x": a(x).reshape(NT, C),
        "ctx_rows": a(ctx_1024).reshape(BATCH * NV, C),
        "mask": a(mask_BxS2xS_ik0).transpose(0, 2, 1).reshape(NB, TB, NV),
        "w_attn": np.stack([a(w) for w in (L0_attn_W1q, L0_attn_W1k, L0_attn_W1v,
                                           L0_attn_W2q, L0_attn_W2k, L0_attn_W2v)], axis=1),
        "cols": np.stack([a(b) for b in (L0_attn_b1q, L0_attn_b1k, L0_attn_b1v, L0_attn_b2q, L0_attn_b2k,
                                         L0_xattn_ln_w, L0_xattn_ln_b)], axis=1),
        "rows": np.stack([a(L0_attn_b2v), a(L0_attn_ln_w), a(L0_attn_ln_b)]),
        "w_x": np.stack([by_heads(a(L0_xattn_Wq).T), by_heads(wkv[:, 0:INNER].T),
                         by_heads(wkv[:, INNER:].T), by_heads(L0_xattn_Wout)], axis=1),
        "w_gate": a(L0_ffn_gate_w),
        "w_ffn": np.stack([a(L0_ffn_w1), a(L0_ffn_w3),
                           a(L0_ffn_w2).reshape(E, FC, 128, C).transpose(0, 2, 1, 3).reshape(E, 128, F)],
                          axis=2),
        "consts": consts,
    }
    arrays = {name: np.ascontiguousarray(v) for name, v in arrays.items()}
    nc = bacc.Bacc("TRN2", target_bir_lowering=False, num_devices=1)
    args = [nc.dram_tensor(name, v.shape, mybir.dt.from_np(v.dtype), kind="ExternalInput").ap()
            for name, v in arrays.items()]
    out = nc.dram_tensor("out", (NT, C), F32, kind="ExternalOutput").ap()
    decoder_layer(nc, *args, out)
    r = run_bass_kernel_spmd(nc, [arrays], core_ids=[0])
    return r.results[0]["out"].reshape(BATCH, SEQ, C)
```

```python
from contextlib import ExitStack

import numpy as np

import concourse.bass as bass
from concourse import mybir

ALU = mybir.AluOpType
ACT = mybir.ActivationFunctionType
AX = mybir.AxisListType
F32 = mybir.dt.float32
F16 = mybir.dt.float16
BF16 = mybir.dt.bfloat16
F32R = mybir.dt.float32r
I32 = mybir.dt.int32
U32 = mybir.dt.uint32

BATCH, SEQ, C = 8, 56, 128
NV = 1500
NB = 4
TB = BATCH * SEQ // NB
NT = BATCH * SEQ
H, DH = 8, 64
KS = 5
GT = 16
GB = TB // GT
G = NB * GB
GR = GT * KS
E, F = 8, 512
FC = F // 128
NCH = E * FC
WS = 6
EARLY = 6
FIRST_LATE = 10
PIECES = 8
PW = 3 * F // PIECES
NS = 4
NH = 6
LAG = 7
BEHIND = 3
U3 = 2
EPS = 1e-5
SCORE_SCALE = float((128.0 * 256.0) ** 0.5)
CG = 6
CHUNKS = [(a, min(a + CG, G)) for a in range(0, G, CG)]
QG = 4
QUADS = G // QG
HALVES = [(0, 2), (2, len(CHUNKS))]


def decoder_layer(nc, x, ctx_rows, mask, w_attn, cols, rows, w_x, w_gate, w_ffn, consts, out):
    with ExitStack() as stack:
        def sb(name, shape, dt=F32):
            return stack.enter_context(nc.sbuf_tensor(name, shape, dt))

        def sem(name):
            return stack.enter_context(nc.semaphore(name))

        bank = [stack.enter_context(nc.psum_tensor(f"bank{i}", [128, 512], F32)) for i in range(8)]

        col = sb("col", [128, 7])
        gate = sb("gate", [C, E])
        gate_hi = sb("gate_hi", [C, E], F32R)
        gate_lo = sb("gate_lo", [C, E], F32R)
        raw = sb("raw", [128, 2, 3 * F])
        cst = sb("cst", [128, 128 + TB + GT + NB + E])
        sel = sb("sel", [2 * E, E, 128], F32R)
        zeros = sb("zeros", [128, NT], BF16)
        unused = sb("unused", [128, 5])
        ident = cst[:, 0:128]
        causal = cst[0:TB, 128:128 + TB]
        own = cst[:, 128 + TB:128 + TB + GT]
        row_base = cst[0:TB, 128 + TB + GT:128 + TB + GT + NB]
        expert_no = cst[0:TB, 128 + TB + GT + NB:128 + TB + GT + NB + E]
        top = sb("top", [TB, NB, 8])
        top16 = sb("top16", [TB, NB, KS], F16)
        rep16 = sb("rep16", [TB, GB, H, GT], F16)
        row_idx = sb("row_idx", [TB, NB, KS], I32)
        keyrep = sb("keyrep", [128, GB, NB, KS])
        valid = sb("valid", [128, G, KS])
        vbias = sb("vbias", [128, G, KS])
        mhalf = sb("mhalf", [TB, NB])
        euler = sb("euler", [TB, NB])
        stats = sb("stats", [TB, NB, 6])
        mv = sb("mv", [TB, NB, 2])
        ve = sb("ve", [TB, NB])
        rstd = sb("rstd", [TB, NB])
        std = sb("std", [TB, NB])
        eps_of = sb("eps_of", [TB, 2])
        xn = sb("xn", [TB, NB, C])
        xnT = sb("xnT", [C, NT])
        on = sb("on", [TB, NB, C])
        xb = sb("xb", [TB, NB, C])
        x1 = sb("x1", [TB, NB, C])
        x2 = xb
        y_out = x1
        aw = sb("aw", [C, H, C])
        mw = sb("mw", [C, H, C])
        simx = sb("simx", [128, 2, CG, KS, GT])
        sim = sb("sim", [128, G, KS])
        s1 = sb("s1", [128, G, KS])
        s2 = sb("s2", [128, G, KS])
        s3 = sb("s3", [128, G, KS])
        ex = sb("ex", [128, G, KS])
        exv = sb("exv", [128, G, KS])
        smax = sb("smax", [128, G])
        ssum = sb("ssum", [128, G])
        srec = sb("srec", [128, G])
        attn = sb("attn", [128, G, KS])
        ltop = sb("ltop", [TB, NB, 8])
        lidx = sb("lidx", [TB, NB, 8], U32)
        lidf = sb("lidf", [TB, NB, 2])
        ld = sb("ld", [TB, NB])
        le = sb("le", [TB, NB])
        lsum = sb("lsum", [TB, NB])
        lw = sb("lw", [TB, NB, 2])
        pick = sb("pick", [TB, NB, 2, E])
        pickw = sb("pickw", [TB, NB, 2, E])
        wi = sb("wi", [TB, NB, E])
        wparts = sb("wparts", [TB, NB, 2, E], F32R)
        wT = sb("wT", [2 * E, NT], F32R)
        yT = sb("yT", [C, NT])
        xnh = sb("xnh", [C, NT], F32R)
        xnl = sb("xnl", [C, NT], F32R)

        with ExitStack() as later:
            sil, gated, hw = (later.enter_context(nc.sbuf_tensor(name, [128, NS, NT], F32))
                              for name in ("sil", "gated", "hw"))
            hh, hl = (later.enter_context(nc.sbuf_tensor(name, [128, NH, NT], F32R)) for name in ("hh", "hl"))
            wb = later.enter_context(nc.sbuf_tensor("wb", [128, 2, NT], F32))
        arena = sb("arena", [128, NB * NV])
        mask_sb = arena[0:TB, :].bitcast(I32).rearrange("p (b v) -> p b v", b=NB)
        attT = arena[0:GR, 0:G * 128].rearrange("p (g r) -> p g r", g=G)
        attx = arena[:, G * 128:G * (128 + GR)].rearrange("p (g k t) -> p g k t", g=G, k=KS)
        cxT = sb("cxT", [C, H, NT])
        vt = (cxT[0:TB, :, :].rearrange("p h n -> p (h n)")[:, 0:NB * KS * C]
              .rearrange("p (b k c) -> p b k c", b=NB, k=KS))
        vgT = sb("vgT", [C, G, KS, GT])
        vg = sb("vg", [GR, G, C])
        qp = sb("qp", [C, G, H, GT])

        with ExitStack() as early:
            def sb_early(name, shape, dt=F32):
                return early.enter_context(nc.sbuf_tensor(name, shape, dt))

            key_w = sb_early("key_w", [TB, NV])
            key = sb_early("key", [TB, 2, NV])
            wx = sb_early("wx", [128, 4, 4, C])
            wa = sb_early("wa", [128, 6, C])
            hid = sb_early("hid", [C, 3, NT])
            x_tok = sb_early("x_tok", [TB, NB, C])
            row = sb_early("row", [TB, 3, C])
            qT = sb_early("qT", [C, NT])
            kT = sb_early("kT", [C, NT])
            v_tok = sb_early("v_tok", [TB, NB, C])
            sT = sb_early("sT", [TB, NB, TB])
        wlo = sb("wlo", [128, WS, 3 * F], F32R)
        whi = sb("whi", [128, WS, 3 * F], F32R)

        x_in = sem("x_in")
        cst_in = sem("cst_in")
        wa_in = sem("wa_in")
        col_in = sem("col_in")
        row_in = sem("row_in")
        mask_in = [sem(f"mask_in{b}") for b in range(NB)]
        wx_in = sem("wx_in")
        gate_in = sem("gate_in")
        raw_in = [sem(f"raw_in{e}") for e in range(E)]
        rows_in = [sem(f"rows_in{b}") for b in range(NB)]
        y_stored = sem("y_stored")
        zeros_ready = sem("zeros_ready")
        sel_ready = sem("sel_ready")
        xb_ready = sem("xb_ready")
        gate_split = sem("gate_split")
        keyw_ready = sem("keyw_ready")
        small_ready = sem("small_ready")
        key_ready = sem("key_ready")
        top_ready = sem("top_ready")
        top16_ready = sem("top16_ready")
        idx_ready = sem("idx_ready")
        keyrep_ps = sem("keyrep_ps")
        keyrep_read = sem("keyrep_read")
        vgT_ps = sem("vgT_ps")
        vgT_ready = sem("vgT_ready")
        vg_ps = sem("vg_ps")
        vg_ready = sem("vg_ready")
        act_small = sem("act_small")
        var_ready = sem("var_ready")
        mv_ready = sem("mv_ready")
        std_ready = sem("std_ready")
        rstd_ready = sem("rstd_ready")
        xn_ready = sem("xn_ready")
        xnT_ps = sem("xnT_ps")
        xnT_ready = sem("xnT_ready")
        h_ps = sem("h_ps")
        hid_ready = sem("hid_ready")
        qkv_ps = sem("qkv_ps")
        qk_ready = sem("qk_ready")
        v_ready = sem("v_ready")
        s_ps = sem("s_ps")
        sT_ready = sem("sT_ready")
        o_ps = sem("o_ps")
        wh_ps = sem("wh_ps")
        wh_ready = sem("wh_ready")
        qp_ps = sem("qp_ps")
        qp_act = sem("qp_act")
        qp_dve = sem("qp_dve")
        sim_ps = sem("sim_ps")
        sim_read = sem("sim_read")
        sim_summed = sem("sim_summed")
        s3_ready = sem("s3_ready")
        ex_ready = sem("ex_ready")
        attn_ready = sem("attn_ready")
        attx_dve = sem("attx_dve")
        attx_pool = sem("attx_pool")
        attT_ps = sem("attT_ps")
        attT_ready = sem("attT_ready")
        cx_ps = sem("cx_ps")
        cx_act = sem("cx_act")
        cx_dve = sem("cx_dve")
        xo_ps = sem("xo_ps")
        logit_ps = sem("logit_ps")
        ld_ready = sem("ld_ready")
        le_ready = sem("le_ready")
        wparts_ready = sem("wparts_ready")
        wT_ps = sem("wT_ps")
        wT_ready = sem("wT_ready")
        wb_ps = sem("wb_ps")
        wb_ready = sem("wb_ready")
        up_ps = sem("up_ps")
        whi_dve = sem("whi_dve")
        whi_act = sem("whi_act")
        wlo_ready = sem("wlo_ready")
        xnh_ready = sem("xnh_ready")
        xnl_ready = sem("xnl_ready")
        sil_ready = sem("sil_ready")
        u3_ready = sem("u3_ready")
        gated_ready = sem("gated_ready")
        hw_ready = sem("hw_ready")
        hh_ready = sem("hh_ready")
        hl_ready = sem("hl_ready")
        down_done = sem("down_done")
        yT_ready = sem("yT_ready")
        y_ps = sem("y_ps")
        y_ready = sem("y_ready")
        dve_done = sem("dve_done")

        BX = [bank[0], bank[1], bank[4], bank[5]]
        BG = [bank[6], bank[7], bank[6], bank[7], bank[6], bank[7], bank[7]]
        BS = [bank[0], bank[1], bank[4], bank[5], bank[2]]
        BA = [bank[3], bank[6]]
        BC = [bank[7], bank[0]]
        BO = [bank[1], bank[4], bank[5], bank[2]]
        BT = [bank[1], bank[3], bank[6], bank[5]]
        UP1 = [bank[0], bank[3], bank[6]]
        UP3 = [bank[7], bank[2], bank[5]]
        Y = bank[1]

        def spread_weights(eng, q):
            return eng.tensor_tensor(attx[:, q * QG:(q + 1) * QG, :, :],
                                     attn[:, q * QG:(q + 1) * QG, :].unsqueeze(3)
                                     .broadcast_to([128, QG, KS, GT]),
                                     own.unsqueeze(1).unsqueeze(1).broadcast_to([128, QG, KS, GT]), ALU.mult)

        WARM_UP = 15
        FILL = 13
        GATED_EARLY = 1
        EARLY_TOKENS = slice(0, (NB - 1) * TB)
        LATE_TOKENS = slice((NB - 1) * TB, NT)
        QUERIES_BY_DVE = [5, 7]
        SPREAD_BY_POOL = [1, 2, 5, 6]
        SPLIT_BY_ACT = [2, 3, 4, 5]
        CONTEXT_BY_ACT = [0, 1, 2, 5]

        def wait_context(eng, q):
            by_act = sum(p <= q for p in CONTEXT_BY_ACT)
            eng.wait_ge(cx_act, by_act)
            if q + 1 > by_act:
                eng.wait_ge(cx_dve, q + 1 - by_act)

        def context_by_head(copy, q):
            t0, t1 = q * QG * GT, (q + 1) * QG * GT
            return copy(cxT[:, :, t0:t1].rearrange("p h (g t) -> p g h t", t=GT),
                        BC[q % 2][:, :].rearrange("p (g h t) -> p g h t", h=H, t=GT))

        WHOLE = [(0, 3 * F)]
        TWO_HALVES = [(0, 3 * F // 2), (3 * F // 2, 3 * F)]
        PARTS = [(p * PW, (p + 1) * PW) for p in range(PIECES)]

        def late_piece(i):
            n = i - FIRST_LATE
            return (EARLY + n // PIECES, n % PIECES) if 0 <= n < (E - EARLY) * PIECES else None

        def weights_beside(i):
            if i == FC:
                return 1
            return i // FC + 1 if i > FC and i % FC == FC - 1 and i // FC + 1 < E else 0

        def lo_count(e):
            return e + 1 + (e >= 4) if e < EARLY else EARLY + 1 + (e - EARLY + 1) * PIECES

        block = stack.enter_context(nc.Block())

        @block.sync
        def _(sp):
            sp.dma_start(x_tok[:, :, :], x.rearrange("(b p) c -> p b c", p=TB)).then_inc(x_in, 16)
            sp.dma_start(mask_sb[:, 0, :], mask[0]).then_inc(mask_in[0], 16)
            sp.dma_start(wa[:, :, :], w_attn).then_inc(wa_in, 16)
            sp.dma_start(mask_sb[:, 1, :], mask[1]).then_inc(mask_in[1], 16)
            sp.dma_start(wx[:, :, :, :], w_x).then_inc(wx_in, 16)
            for b in range(2, NB):
                sp.dma_start(mask_sb[:, b, :], mask[b]).then_inc(mask_in[b], 16)
            sp.dma_start(gate[:, :], w_gate).then_inc(gate_in, 16)
            for e in range(E):
                if e < 2:
                    sp.wait_ge(rows_in[e], 16 * KS)
                if e >= 2:
                    sp.wait_ge(wlo_ready, lo_count(e - 2))
                sp.dma_start(raw[:, e % 2, :], w_ffn[e]).then_inc(raw_in[e], 16)
            for n in range(2):
                sp.wait_ge(y_ready, n + 1)
                sp.dma_start(out.rearrange("(b p) c -> p b c", p=TB)[:, 2 * n:2 * n + 2, :],
                             y_out[:, 2 * n:2 * n + 2, :]).then_inc(y_stored, 16)
            sp.wait_ge(y_stored, 32)

        @block.gpsimd
        def _(pool):
            pool.memset(mhalf[:, :], -0.5)
            pool.memset(euler[:, :], float(np.e))
            pool.memset(eps_of[:, 0:1], EPS)
            pool.memset(eps_of[:, 1:2], EPS * EPS).then_inc(small_ready, 1)
            pool.iota(key_w[:, :], [[-1, NV]], base=NV, channel_multiplier=0,
                      allow_small_or_imprecise_dtypes=True).then_inc(keyw_ready, 1)

            def rsqrt(b):
                pool.wait_ge(var_ready, b + 1)
                pool.tensor_tensor(rstd[:, b:b + 1], ve[:, b:b + 1], mhalf[:, b:b + 1],
                                   ALU.pow).then_inc(rstd_ready, 1)

            pool.wait_ge(x_in, 16)
            pool.wait_ge(row_in, 16)
            pool.tensor_tensor(xb[:, :, :], x_tok[:, :, :], row[:, 2, :].unsqueeze(1).broadcast_to([TB, NB, C]),
                               ALU.add).then_inc(xb_ready, 1)
            pool.wait_ge(cst_in, 16)
            pool.tensor_tensor(sel[:, :, :], ident[0:2 * E, 0:E].unsqueeze(2).broadcast_to([2 * E, E, 128]),
                               ident[0:2 * E, E:2 * E].unsqueeze(2).broadcast_to([2 * E, E, 128]),
                               ALU.add).then_inc(sel_ready, 1)
            for j in range(NB * KS):
                b, k = j // KS, j % KS
                if k == 0:
                    pool.wait_ge(idx_ready, b + 1)
                pool.indirect_dma_start(
                    out=vt[:, b, k, :], out_offset=None, in_=ctx_rows,
                    in_offset=bass.IndirectOffsetOnAxis(ap=row_idx[:, b, k:k + 1], axis=0),
                ).then_inc(rows_in[b], 16)

            def split_low(e, p, a, z):
                if e in SPLIT_BY_ACT:
                    pool.wait_ge(whi_act, SPLIT_BY_ACT.index(e) + 1)
                else:
                    pool.wait_ge(whi_dve, e + 1 if e < EARLY else
                                 EARLY - len(SPLIT_BY_ACT) + (e - EARLY) * PIECES + p + 1)
                pool.tensor_tensor(wlo[:, e % WS, a:z], raw[:, e % 2, a:z],
                                   whi[:, e % WS, a:z].bitcast(F32), ALU.subtract).then_inc(wlo_ready, 1)

            split_low(0, 0, *WHOLE[0])
            for q in SPREAD_BY_POOL[0:2]:
                pool.wait_ge(attn_ready, 1)
                spread_weights(pool, q).then_inc(attx_pool, 1)
            split_low(1, 0, *WHOLE[0])
            for q in SPREAD_BY_POOL[2:4]:
                pool.wait_ge(attn_ready, 2)
                spread_weights(pool, q).then_inc(attx_pool, 1)
            split_low(2, 0, *WHOLE[0])
            pool.wait_ge(small_ready, 1)
            rsqrt(0)
            split_low(3, 0, *WHOLE[0])
            rsqrt(1)
            rsqrt(2)
            split_low(4, 0, *TWO_HALVES[0])
            rsqrt(3)
            split_low(4, 0, *TWO_HALVES[1])
            pool.wait_ge(ld_ready, 1)
            pool.tensor_tensor(le[:, :], euler[:, :], ld[:, :], ALU.pow).then_inc(le_ready, 1)
            split_low(5, 0, *WHOLE[0])
            for i in range(NCH):
                e = i // FC
                pool.wait_ge(wb_ready, e + 1)
                if i >= NS:
                    pool.wait_ge(hl_ready, i - NS + 1)
                pool.wait_ge(gated_ready, i + 1)
                pool.tensor_tensor(hw[:, i % NS, :], gated[:, i % NS, :], wb[:, e % 2, :],
                                   ALU.mult).then_inc(hw_ready, 1)
                if late_piece(i):
                    split_low(*late_piece(i), *PARTS[late_piece(i)[1]])

        @block.scalar
        def _(act):
            act.dma_start(cst[:, :], consts).then_inc(cst_in, 16)
            act.dma_start(col[:, :], cols).then_inc(col_in, 16)
            act.dma_start(row[:, :, :], rows.partition_broadcast(TB)).then_inc(row_in, 16)

            def deviation(n, eps, scale):
                act.wait_ge(mv_ready, n)
                act.activation(std[:, :], mv[:, :, 1], ACT.Sqrt, bias=eps_of[:, eps:eps + 1],
                               scale=scale).then_inc(std_ready, 1)

            act.wait_ge(zeros_ready, 1)
            act.activation(unused[:, 4:5], zeros[:, 0:1], ACT.Sqrt)
            act.wait_ge(small_ready, 1)
            deviation(1, 0, 1.0)
            act.activation(unused[:, 0:1], zeros[:, 0:1], ACT.Gelu)
            act.wait_ge(cst_in, 16)
            act.copy(rep16[:, :, :, :], ident[0:TB, 0:TB].rearrange("p (i t) -> p i t", t=GT).unsqueeze(2)
                     .broadcast_to([TB, GB, H, GT])).then_inc(act_small, 1)
            act.wait_ge(col_in, 16)
            act.wait_ge(xnT_ps, 1)
            act.copy(xnT[:, :], bank[0][:, 0:NT]).then_inc(xnT_ready, 1)
            for n in range(3):
                act.wait_ge(h_ps, n + 1)
                act.activation(hid[:, n, :], bank[1 + n][:, 0:NT], ACT.Gelu,
                               bias=col[:, n:n + 1]).then_inc(hid_ready, 1)
            for n, dst in enumerate([qT, kT]):
                act.wait_ge(qkv_ps, n + 1)
                act.activation(dst[:, :], bank[4 + n][:, 0:NT], ACT.Identity,
                               bias=col[:, 3 + n:4 + n]).then_inc(qk_ready, 1)
            act.activation(unused[:, 2:3], zeros[:, 0:1], ACT.Sqrt)

            def head_weights(n):
                act.wait_ge(wh_ps, n + 1)
                act.mul((aw if n < 2 else mw)[:, n % 2:H:2, :],
                        bank[4 + n % 2][:, :].rearrange("p (j c) -> p j c", c=C),
                        DH ** -0.5 if n < 2 else 1.0).then_inc(wh_ready, 1)

            head_weights(0)
            head_weights(1)
            deviation(2, 0, 1.0)
            head_weights(2)
            head_weights(3)

            def rows_channels_first(b):
                for i, (k0, k1) in enumerate([(0, 4), (4, KS)]):
                    act.wait_ge(vgT_ps, 2 * b + i + 1)
                    act.copy(vgT[:, b * GB:(b + 1) * GB, k0:k1, :].rearrange("p g k t -> p k g t"),
                             bank[2 + i][:, 0:(k1 - k0) * TB].rearrange("p (k g t) -> p k g t", g=GB, t=GT)
                             ).then_inc(vgT_ready, 1)

            def rows_by_group(q):
                act.wait_ge(vg_ps, q + 1)
                act.copy(vg[:, q * QG:(q + 1) * QG, :].rearrange("p g c -> p (g c)"),
                         BG[q][0:GR, :]).then_inc(vg_ready, 1)

            rows_channels_first(0)
            rows_by_group(0)
            deviation(3, 1, 1.0 + EPS)
            act.wait_ge(xnT_ps, 2)
            act.activation(xnT[:, :], bank[0][:, 0:NT], ACT.Identity, bias=col[:, 6:7],
                           scale=col[:, 5:6]).then_inc(xnT_ready, 1)
            rows_channels_first(1)
            for h in range(H):
                if h not in QUERIES_BY_DVE:
                    act.wait_ge(qp_ps, h + 1)
                    act.copy(qp[:, :, h, :], BX[h % 4][:, 0:NT].rearrange("p (g t) -> p g t", t=GT)
                             ).then_inc(qp_act, 1)
                if h in (1, 3):
                    rows_by_group((h + 1) // 2)
            rows_channels_first(2)
            act.activation(unused[:, 1:2], zeros[:, 0:1], ACT.Exp)
            rows_by_group(3)
            rows_channels_first(3)

            def exponentials(n):
                g0, g1 = CHUNKS[HALVES[n][0]][0], CHUNKS[HALVES[n][1] - 1][1]
                act.wait_ge(s3_ready, n + 1)
                act.activation(ex[:, g0:g1, :], s3[:, g0:g1, :], ACT.Exp).then_inc(ex_ready, 1)

            def weights_by_row(q):
                act.wait_ge(attT_ps, q + 1)
                act.copy(attT[:, q * QG:(q + 1) * QG, :].rearrange("p g r -> p (g r)"),
                         BA[q % 2][0:GR, :]).then_inc(attT_ready, 1)

            def context(q):
                act.wait_ge(cx_ps, q + 1)
                context_by_head(act.copy, q).then_inc(cx_act, 1)

            def split_high(e):
                act.wait_ge(raw_in[e], 16)
                act.copy(whi[:, e % WS, :], raw[:, e % 2, :]).then_inc(whi_act, 1)

            def tokens_high(b):
                act.wait_ge(xnT_ps, 3 + b)
                act.copy(xnh[:, b * TB:(b + 1) * TB], BT[b][:, 0:TB]).then_inc(xnh_ready, 1)

            exponentials(0)
            rows_by_group(4)
            weights_by_row(0)
            rows_by_group(5)
            weights_by_row(1)
            weights_by_row(2)
            context(0)
            context(1)
            exponentials(1)
            context(2)
            split_high(2)
            weights_by_row(3)
            weights_by_row(4)
            rows_by_group(6)
            weights_by_row(5)
            split_high(3)
            tokens_high(0)
            weights_by_row(6)
            context(5)
            split_high(4)
            tokens_high(1)
            act.activation(unused[:, 3:4], zeros[:, 0:1], ACT.Silu)
            tokens_high(2)
            tokens_high(3)
            split_high(5)

            def weight_copy(e):
                act.wait_ge(wb_ps, e + 1)
                if e >= 2:
                    act.wait_ge(hw_ready, FC * (e - 1))
                act.copy(wb[:, e % 2, :], bank[4][:, 0:NT]).then_inc(wb_ready, 1)

            def silu(i):
                if i >= NS:
                    act.wait_ge(gated_ready, i - NS + 1)
                act.wait_ge(up_ps, 2 * i + 1)
                act.activation(sil[:, i % NS, :], UP1[i % 3][:, 0:NT], ACT.Silu).then_inc(sil_ready, 1)

            def hidden_high(i):
                if i >= NH:
                    act.wait_ge(down_done, i - NH + 1)
                act.wait_ge(hw_ready, i + 1)
                act.copy(hh[:, i % NH, :], hw[:, i % NS, :]).then_inc(hh_ready, 1)

            for i in range(U3):
                silu(i)
                act.wait_ge(up_ps, 2 * i + 2)
                act.copy(hw[:, i, :], UP3[i][:, 0:NT]).then_inc(u3_ready, 1)
            for i in range(U3, 4):
                silu(i)
            weight_copy(0)
            for i in range(4, NCH + BEHIND + 1):
                hidden_high(i - BEHIND - 1)
                if i < NCH:
                    silu(i)
                    if weights_beside(i):
                        weight_copy(weights_beside(i))

        @block.vector
        def _(dve):
            chain = [0]

            def then(ins):
                chain[0] += 1
                ins.then_inc(dve_done, 1)
                dve.wait_ge(dve_done, chain[0])

            def mark_rows(b):
                if b == 0:
                    dve.wait_ge(keyw_ready, 1)
                dve.wait_ge(mask_in[b], 16)
                dve.scalar_tensor_tensor(out=key[:, b % 2, :], in0=mask_sb[:, b, :], scalar=0.0,
                                         in1=key_w[:, :], op0=ALU.not_equal,
                                         op1=ALU.mult).then_inc(key_ready, 1)

            def index_rows(b):
                dve.wait_ge(key_ready, b + 1)
                dve.max(top[:, b, :], key[:, b % 2, :]).then_inc(top_ready, 1)
                dve.wait_ge(top_ready, b + 1)
                dve.scalar_tensor_tensor(out=row_idx[:, b, :], in0=top[:, b, 0:KS], scalar=1.0,
                                         in1=row_base[:, b:b + 1].broadcast_to([TB, KS]), op0=ALU.max,
                                         op1=ALU.subtract, reverse1=True).then_inc(idx_ready, 1)

            def variance(src, b0=0, b1=NB, n=0):
                for b in range(b0, b1):
                    last = dve.bn_stats(stats[:, b, :], src[:, b, :])
                then(last)
                for b in range(b0, b1):
                    last = dve.bn_aggr(mv[:, b, :], stats[:, b, :])
                if n:
                    last.then_inc(mv_ready, 1)
                    dve.wait_ge(mv_ready, n)
                else:
                    then(last)

            def inverse(n):
                dve.wait_ge(std_ready, n)
                then(dve.reciprocal(rstd[:, :], std[:, :]))

            def variance_eps(b):
                dve.tensor_scalar(ve[:, b:b + 1], mv[:, b:b + 1, 1], EPS, None, ALU.add).then_inc(var_ready, 1)

            def normalise(dst, src, b0=0, b1=NB):
                for b in range(b0, b1):
                    dve.tensor_scalar(dst[:, b, :], src[:, b, :], mv[:, b, 0:1], rstd[:, b:b + 1],
                                      ALU.subtract, ALU.mult).then_inc(xn_ready, 1)

            def blocks(ap, n):
                return ap.unsqueeze(1).broadcast_to([ap.shape[0], n, ap.shape[1]])

            dve.memset(zeros[:, :], 0.0).then_inc(zeros_ready, 1)
            dve.wait_ge(x_in, 16)
            variance(x_tok, n=1)
            inverse(1)
            normalise(xn, x_tok)
            dve.wait_ge(cst_in, 16)
            mark_rows(0)
            index_rows(0)
            mark_rows(1)
            index_rows(1)
            dve.wait_ge(row_in, 16)
            dve.wait_ge(qkv_ps, 3)
            dve.tensor_tensor(v_tok[:, :, :], bank[6][0:TB, :].rearrange("p (b c) -> p b c", b=NB),
                              blocks(row[:, 0, :], NB), ALU.add).then_inc(v_ready, 1)
            dve.wait_ge(s_ps, 1)
            dve.tensor_tensor(sT[:, :, :], bank[0][0:TB, 0:NB * TB].rearrange("p (b c) -> p b c", b=NB),
                              blocks(causal, NB), ALU.mult).then_inc(sT_ready, 1)
            mark_rows(2)
            dve.wait_ge(o_ps, 1)
            o_tok = bank[1][0:TB, :].rearrange("p (b c) -> p b c", b=NB)
            variance(o_tok, n=2)
            for b in range(NB):
                last = dve.scalar_tensor_tensor(out=on[:, b, :], in0=o_tok[:, b, :], scalar=mv[:, b, 0:1],
                                                in1=row[:, 1, :], op0=ALU.subtract, op1=ALU.mult)
            inverse(2)
            dve.wait_ge(xb_ready, 1)
            for b in range(NB):
                last = dve.scalar_tensor_tensor(out=x1[:, b, :], in0=on[:, b, :], scalar=rstd[:, b:b + 1],
                                                in1=xb[:, b, :], op0=ALU.mult, op1=ALU.add)
            then(last)
            variance(x1, n=3)
            inverse(3)
            normalise(xn, x1)
            index_rows(2)
            mark_rows(3)
            index_rows(3)
            dve.tensor_copy(top16[:, :, :], top[:, :, 0:KS]).then_inc(top16_ready, 1)

            def split_high(e, a, z):
                dve.wait_ge(raw_in[e], 16)
                if e >= WS:
                    dve.wait_ge(down_done, FC * (e - WS + 1))
                dve.tensor_copy(whi[:, e % WS, a:z], raw[:, e % 2, a:z]).then_inc(whi_dve, 1)

            dve.wait_ge(gate_in, 16)
            dve.tensor_copy(gate_hi[:, :], gate[:, :]).then_inc(gate_split, 1)
            dve.wait_ge(gate_split, 1)
            dve.tensor_tensor(gate_lo[:, :], gate[:, :], gate_hi[:, :].bitcast(F32),
                              ALU.subtract).then_inc(gate_split, 1)
            for h in QUERIES_BY_DVE:
                dve.wait_ge(qp_ps, h + 1)
                dve.tensor_copy(qp[:, :, h, :], BX[h % 4][:, 0:NT].rearrange("p (g t) -> p g t", t=GT)
                                ).then_inc(qp_dve, 1)
                if h == 5:
                    dve.wait_ge(keyrep_ps, 1)
                    dve.tensor_copy(keyrep[:, :, :, :].rearrange("p i b k -> p (i b k)"),
                                    bank[6][:, 0:GB * NB * KS]).then_inc(keyrep_read, 1)
                    dve.wait_ge(keyrep_read, 1)
                    then(dve.tensor_scalar(valid[:, :, :].rearrange("p (b i) k -> p b i k", b=NB),
                                           keyrep[:, :, :, :].rearrange("p i b k -> p b i k"), 1.0, None, ALU.min))
                    dve.tensor_scalar(vbias[:, :, :], valid[:, :, :], 10000.0, -10000.0, ALU.mult, ALU.add)
            split_high(0, *WHOLE[0])
            split_high(1, *WHOLE[0])

            def own_scores(c0, c1):
                for c in range(c0, c1 + 1):
                    if c < c1:
                        a, z = CHUNKS[c]
                        dve.wait_ge(sim_ps, c + 1)
                        if c >= 2:
                            dve.wait_ge(sim_summed, c - 1)
                        dve.tensor_tensor(simx[:, c % 2, 0:z - a, :, :],
                                          BS[c][:, 0:(z - a) * GR].rearrange("p (g k t) -> p g k t", t=GT, k=KS),
                                          own.unsqueeze(1).unsqueeze(1).broadcast_to([128, z - a, KS, GT]),
                                          ALU.mult).then_inc(sim_read, 1)
                    if c > c0:
                        a, z = CHUNKS[c - 1]
                        dve.wait_ge(sim_read, c)
                        dve.tensor_reduce(sim[:, a:z, :], simx[:, (c - 1) % 2, 0:z - a, :, :],
                                          AX.X, ALU.add).then_inc(sim_summed, 1)
                dve.wait_ge(sim_summed, c1)

            def softmax(n):
                g0, g1 = CHUNKS[HALVES[n][0]][0], CHUNKS[HALVES[n][1] - 1][1]
                g = slice(g0, g1)

                def over_rows(ap):
                    return ap[:, g].unsqueeze(2).broadcast_to([128, g1 - g0, KS])

                then(dve.tensor_tensor(s1[:, g, :], sim[:, g, :], valid[:, g, :], ALU.mult))
                then(dve.tensor_tensor(s2[:, g, :], s1[:, g, :], vbias[:, g, :], ALU.add))
                then(dve.tensor_reduce(smax[:, g], s2[:, g, :], AX.X, ALU.max))
                dve.tensor_tensor(s3[:, g, :], s2[:, g, :], over_rows(smax), ALU.subtract
                                  ).then_inc(s3_ready, 1)
                dve.wait_ge(ex_ready, n + 1)
                then(dve.tensor_reduce(ssum[:, g], ex[:, g, :], AX.X, ALU.add))
                dve.reciprocal(srec[:, g], ssum[:, g])
                then(dve.tensor_tensor(exv[:, g, :], ex[:, g, :], valid[:, g, :], ALU.mult))
                dve.tensor_tensor(attn[:, g, :], exv[:, g, :], over_rows(srec), ALU.mult
                                  ).then_inc(attn_ready, 1)
                dve.wait_ge(attn_ready, n + 1)
                for q in range(g0 // QG, g1 // QG):
                    if q not in SPREAD_BY_POOL:
                        spread_weights(dve, q).then_inc(attx_dve, 1)

            for n, (c0, c1) in enumerate(HALVES):
                own_scores(c0, c1)
                softmax(n)

            def context(q):
                dve.wait_ge(cx_ps, q + 1)
                context_by_head(dve.tensor_copy, q).then_inc(cx_dve, 1)

            def add_context(b):
                dve.wait_ge(xo_ps, b + 1)
                then(dve.tensor_tensor(x2[:, b, :], x1[:, b, :], BO[b][0:TB, 0:C], ALU.add))
                variance(x2, b, b + 1)
                variance_eps(b)

            def norm_context(b):
                dve.wait_ge(rstd_ready, 1 + b)
                normalise(xn, x2, b, b + 1)

            def tokens_low(b):
                t = slice(b * TB, (b + 1) * TB)
                dve.wait_ge(xnh_ready, b + 1)
                dve.tensor_tensor(xnl[:, t], BT[b][:, 0:TB], xnh[:, t].bitcast(F32),
                                  ALU.subtract).then_inc(xnl_ready, 1)

            context(3)
            add_context(0)
            context(4)
            norm_context(0)
            add_context(1)
            context(6)
            norm_context(1)
            tokens_low(0)
            add_context(2)
            norm_context(2)
            tokens_low(1)
            add_context(3)
            tokens_low(2)
            norm_context(3)
            tokens_low(3)

            def gate_hidden(i):
                if i >= NS:
                    dve.wait_ge(hw_ready, i - NS + 1)
                if i < U3:
                    dve.wait_ge(u3_ready, i + 1)
                else:
                    dve.wait_ge(up_ps, 2 * i + 2)
                dve.wait_ge(sil_ready, i + 1)
                dve.tensor_tensor(gated[:, i % NS, :], sil[:, i % NS, :],
                                  hw[:, i, :] if i < U3 else UP3[i % 3][:, 0:NT],
                                  ALU.mult).then_inc(gated_ready, 1)

            dve.wait_ge(logit_ps, NB)
            logits = bank[4][0:TB, 0:NB * E].rearrange("p (b e) -> p b e", b=NB)
            for b in range(NB):
                last = dve.max(ltop[:, b, :], logits[:, b, :])
            then(last)
            dve.tensor_tensor(ld[:, :], ltop[:, :, 1], ltop[:, :, 0], ALU.subtract).then_inc(ld_ready, 1)
            for b in range(NB):
                last = dve.max_index(lidx[:, b, :], ltop[:, b, :], logits[:, b, :])
            then(last)
            then(dve.tensor_copy(lidf[:, :, :], lidx[:, :, 0:2]))
            dve.tensor_tensor(pick[:, :, :, :],
                              expert_no.unsqueeze(1).unsqueeze(1).broadcast_to([TB, NB, 2, E]),
                              lidf[:, :, :].unsqueeze(3).broadcast_to([TB, NB, 2, E]), ALU.is_equal)
            dve.wait_ge(le_ready, 1)
            then(dve.tensor_scalar(lsum[:, :], le[:, :], 1.0, None, ALU.add))
            then(dve.reciprocal(lw[:, :, 0], lsum[:, :]))
            then(dve.tensor_tensor(lw[:, :, 1], le[:, :], lw[:, :, 0], ALU.mult))
            then(dve.tensor_tensor(pickw[:, :, :, :], pick[:, :, :, :],
                                   lw[:, :, :].unsqueeze(3).broadcast_to([TB, NB, 2, E]), ALU.mult))
            then(dve.tensor_tensor(wi[:, :, :], pickw[:, :, 0, :], pickw[:, :, 1, :], ALU.add))
            then(dve.tensor_copy(wparts[:, :, 0, :], wi[:, :, :]))
            dve.tensor_tensor(wparts[:, :, 1, :], wi[:, :, :], wparts[:, :, 0, :].bitcast(F32),
                              ALU.subtract).then_inc(wparts_ready, 1)
            for i in range(GATED_EARLY):
                gate_hidden(i)
            dve.wait_ge(wT_ps, 1)
            dve.tensor_copy(wT[:, :], bank[4][0:2 * E, 0:NT]).then_inc(wT_ready, 1)
            for i in range(GATED_EARLY, BEHIND):
                gate_hidden(i)
            for i in range(BEHIND, NCH + BEHIND):
                if i < NCH:
                    gate_hidden(i)
                j = i - BEHIND
                dve.wait_ge(hh_ready, j + 1)
                dve.tensor_tensor(hl[:, j % NH, :], hw[:, j % NS, :], hh[:, j % NH, :].bitcast(F32),
                                  ALU.subtract).then_inc(hl_ready, 1)
                if late_piece(i):
                    split_high(late_piece(i)[0], *PARTS[late_piece(i)[1]])
            dve.wait_ge(down_done, NCH)
            for n in range(2):
                t = slice(n * NT // 2, (n + 1) * NT // 2)
                dve.tensor_copy(yT[:, t], Y[:, t]).then_inc(yT_ready, 1)
            for n in range(2):
                b = slice(2 * n, 2 * n + 2)
                dve.wait_ge(y_ps, n + 1)
                dve.tensor_tensor(y_out[:, b, :], x2[:, b, :],
                                  bank[4 + n][0:TB, 0:2 * C].rearrange("p (b c) -> p b c", b=2),
                                  ALU.add).then_inc(y_ready, 1)

        @block.tensor
        def _(pe):
            def turn_tokens(n):
                for b in range(NB):
                    pe.wait_ge(xn_ready, n * NB + b + 1)
                    last = pe.transpose(bank[0][:, b * TB:(b + 1) * TB], xn[:, b, :], ident[0:TB, 0:TB])
                last.then_inc(xnT_ps, 1)

            def keep_warm(b, n):
                for _ in range(n):
                    pe.matmul(bank[b][:, 0:NT], zeros[:, 0:128], zeros[:, :], start=True, stop=True)

            pe.wait_ge(zeros_ready, 1)
            keep_warm(7, WARM_UP)
            pe.wait_ge(cst_in, 16)
            turn_tokens(0)
            pe.wait_ge(wa_in, 16)
            pe.wait_ge(xnT_ready, 1)
            for n in range(3):
                pe.matmul(bank[1 + n][:, 0:NT], wa[:, n, :], xnT[:, :], start=True, stop=True).then_inc(h_ps, 1)
            for n in range(2):
                pe.wait_ge(hid_ready, n + 1)
                pe.matmul(bank[4 + n][:, 0:NT], wa[:, 3 + n, :], hid[:, n, :],
                          start=True, stop=True).then_inc(qkv_ps, 1)
            pe.wait_ge(hid_ready, 3)
            for b in range(NB):
                last = pe.matmul(bank[6][0:TB, b * C:(b + 1) * C], hid[:, 2, b * TB:(b + 1) * TB],
                                 wa[:, 5, :], start=True, stop=True)
            last.then_inc(qkv_ps, 1)
            pe.wait_ge(qk_ready, 2)
            for b in range(NB):
                t = slice(b * TB, (b + 1) * TB)
                last = pe.matmul(bank[0][0:TB, t], kT[:, t], qT[:, t], start=True, stop=True)
            last.then_inc(s_ps, 1)
            pe.wait_ge(wx_in, 16)

            def head_weights(n):
                if n >= 2:
                    pe.wait_ge(wh_ready, n - 1)
                p = slice(DH * (n % 2), DH * (n % 2) + DH)
                for j in range(4):
                    last = pe.matmul(bank[4 + n % 2][:, j * C:(j + 1) * C],
                                     wx[p, 2 * (n // 2), j, :], wx[p, 2 * (n // 2) + 1, j, :],
                                     start=True, stop=True)
                last.then_inc(wh_ps, 1)

            head_weights(0)
            pe.wait_ge(v_ready, 1)
            pe.wait_ge(sT_ready, 1)
            for b in range(NB):
                last = pe.matmul(bank[1][0:TB, b * C:(b + 1) * C], sT[:, b, :], v_tok[:, b, :],
                                 start=True, stop=True)
            last.then_inc(o_ps, 1)
            for n in range(1, 4):
                head_weights(n)

            def rows_channels_first(b):
                pe.wait_ge(rows_in[b], 16 * KS)
                for i, (k0, k1) in enumerate([(0, 4), (4, KS)]):
                    if b >= 1:
                        pe.wait_ge(vgT_ready, 2 * (b - 1) + i + 1)
                    for k in range(k0, k1):
                        last = pe.transpose(bank[2 + i][:, (k - k0) * TB:(k - k0 + 1) * TB], vt[:, b, k, :],
                                            ident[0:TB, 0:TB])
                    last.then_inc(vgT_ps, 1)

            def rows_by_group(q):
                pe.wait_ge(vgT_ready, 2 * (((q + 1) * QG - 1) // GB + 1))
                if q == QUADS - 1:
                    wait_context(pe, 2)
                elif q >= 2:
                    pe.wait_ge(vg_ready, q - 1)
                for j in range(QG):
                    last = pe.transpose(BG[q][0:GR, j * C:(j + 1) * C],
                                        vgT[:, q * QG + j, :, :].rearrange("p k t -> p (k t)"), ident)
                last.then_inc(vg_ps, 1)

            rows_channels_first(0)
            rows_by_group(0)
            keep_warm(7, FILL)
            turn_tokens(1)
            rows_channels_first(1)
            pe.wait_ge(wh_ready, 4)
            pe.wait_ge(xnT_ready, 2)
            for h in range(H):
                if h >= 4:
                    pe.wait_ge(qp_act, h - 3)
                pe.matmul(BX[h % 4][:, 0:NT], aw[:, h, :], xnT[:, :], start=True, stop=True).then_inc(qp_ps, 1)
                if h in (1, 3):
                    rows_by_group((h + 1) // 2)
                if h == 5:
                    pe.wait_ge(act_small, 1)
                    pe.wait_ge(top16_ready, 1)
                    pe.wait_ge(vg_ready, 3)
                    for i in range(GB):
                        last = pe.matmul(bank[6][:, i * NB * KS:(i + 1) * NB * KS],
                                         rep16[:, i, :, :].rearrange("p h t -> p (h t)"),
                                         top16[:, :, :], start=True, stop=True)
                    last.then_inc(keyrep_ps, 1)
            rows_channels_first(2)
            pe.wait_ge(qp_act, H - len(QUERIES_BY_DVE))
            pe.wait_ge(qp_dve, len(QUERIES_BY_DVE))
            for c, (a, z) in enumerate(CHUNKS):
                b = (z - 1) // GB
                if b == NB - 1 and (a - 1) // GB < b:
                    pe.wait_ge(keyrep_read, 1)
                    rows_by_group(3)
                    rows_channels_first(b)
                    rows_by_group(4)
                pe.wait_ge(vgT_ready, 2 * (b + 1))
                for g in range(a, z):
                    last = pe.matmul(BS[c][:, (g - a) * GR:(g - a + 1) * GR],
                                     qp[:, g, :, :].rearrange("p h t -> p (h t)"),
                                     vgT[:, g, :, :].rearrange("p k t -> p (k t)"), start=True, stop=True)
                last.then_inc(sim_ps, 1)

            def weights_by_row(q):
                if q in SPREAD_BY_POOL:
                    pe.wait_ge(attx_pool, SPREAD_BY_POOL.index(q) + 1)
                else:
                    pe.wait_ge(attx_dve, q + 1 - sum(p < q for p in SPREAD_BY_POOL))
                if q >= 2:
                    pe.wait_ge(attT_ready, q - 1)
                for j in range(QG):
                    last = pe.transpose(BA[q % 2][0:GR, j * 128:(j + 1) * 128],
                                        attx[:, q * QG + j, :, :].rearrange("p k t -> p (k t)"), ident)
                last.then_inc(attT_ps, 1)

            def context(q):
                pe.wait_ge(attT_ready, q + 1)
                if q >= 2:
                    wait_context(pe, q - 2)
                for j in range(QG):
                    g = q * QG + j
                    last = pe.matmul(BC[q % 2][:, j * 128:(j + 1) * 128], vg[:, g, :], attT[:, g, :],
                                     start=True, stop=True)
                last.then_inc(cx_ps, 1)

            def output(b):
                wait_context(pe, ((b + 1) * GB - 1) // QG)
                for h in range(H):
                    last = pe.matmul(BO[b][0:TB, 0:C], cxT[:, h, b * TB:(b + 1) * TB],
                                     mw[:, h, :], start=(h == 0), stop=(h == H - 1))
                last.then_inc(xo_ps, 1)

            def turn_block(b):
                pe.wait_ge(xn_ready, 2 * NB + b + 1)
                pe.transpose(BT[b][:, 0:TB], xn[:, b, :], ident[0:TB, 0:TB]).then_inc(xnT_ps, 1)

            def logits(b):
                pe.wait_ge(gate_split, 2)
                pe.wait_ge(xnl_ready, b + 1)
                t = slice(b * TB, (b + 1) * TB)
                part = bank[4][0:TB, b * E:(b + 1) * E]
                pe.matmul(part, xnh[:, t], gate_hi[:, :], start=True, stop=False)
                pe.matmul(part, xnh[:, t], gate_lo[:, :], start=False, stop=False)
                pe.matmul(part, xnl[:, t], gate_hi[:, :], start=False, stop=True).then_inc(logit_ps, 1)

            def product_high(out, part, e, c, high, start):
                w = slice(part * F + c * 128, part * F + (c + 1) * 128)
                pe.matmul(out, whi[:, e % WS, w], high, start=start, stop=False, skip_group_check=True)
                pe.matmul(out, wlo[:, e % WS, w], high, start=False, stop=False, skip_group_check=True)

            def product_low(out, part, e, c, low, stop):
                w = slice(part * F + c * 128, part * F + (c + 1) * 128)
                return pe.matmul(out, whi[:, e % WS, w], low, start=False, stop=stop, skip_group_check=True)

            def product(out, part, e, c, high, low, start, stop):
                product_high(out, part, e, c, high, start)
                return product_low(out, part, e, c, low, stop)

            def up_w1(i, t=slice(0, NT)):
                if i % FC == 0:
                    pe.wait_ge(wlo_ready, lo_count(i // FC))
                if i >= 3:
                    pe.wait_ge(sil_ready, i - 2)
                last = product(UP1[i % 3][:, t], 0, i // FC, i % FC, xnh[:, t], xnl[:, t], True, True)
                if t.stop == NT:
                    last.then_inc(up_ps, 1)

            def up_w3(i, t=slice(0, NT)):
                if 3 <= i < 3 + U3:
                    pe.wait_ge(u3_ready, i - 2)
                elif i >= 3:
                    pe.wait_ge(gated_ready, i - 2)
                last = product(UP3[i % 3][:, t], 1, i // FC, i % FC, xnh[:, t], xnl[:, t], True, True)
                if t.stop == NT:
                    last.then_inc(up_ps, 1)

            weights_by_row(0)
            rows_by_group(5)
            pe.wait_ge(vg_ready, 5)
            weights_by_row(1)
            weights_by_row(2)
            pe.wait_ge(vg_ready, 6)
            context(0)
            context(1)
            context(2)
            output(0)
            weights_by_row(3)
            weights_by_row(4)
            rows_by_group(6)
            context(3)
            weights_by_row(5)
            pe.wait_ge(vg_ready, QUADS)
            context(4)
            output(1)
            turn_block(0)
            weights_by_row(6)
            context(5)
            context(6)
            output(2)
            turn_block(1)
            logits(0)
            output(3)
            turn_block(2)
            logits(1)
            pe.wait_ge(wlo_ready, 1)
            pe.wait_ge(xnh_ready, 3)
            product_high(UP1[0][:, EARLY_TOKENS], 0, 0, 0, xnh[:, EARLY_TOKENS], True)
            product_high(UP3[0][:, EARLY_TOKENS], 1, 0, 0, xnh[:, EARLY_TOKENS], True)
            logits(2)
            product_low(UP1[0][:, EARLY_TOKENS], 0, 0, 0, xnl[:, EARLY_TOKENS], True)
            product_low(UP3[0][:, EARLY_TOKENS], 1, 0, 0, xnl[:, EARLY_TOKENS], True)
            turn_block(3)
            up_w1(1, EARLY_TOKENS)
            up_w3(1, EARLY_TOKENS)
            logits(3)
            for i in range(2):
                up_w1(i, LATE_TOKENS)
                up_w3(i, LATE_TOKENS)

            def down(i):
                pe.wait_ge(hl_ready, i + 1)
                product(Y[:, 0:NT], 2, i // FC, i % FC, hh[:, i % NH, :], hl[:, i % NH, :],
                        i == 0, i == NCH - 1).then_inc(down_done, 1)

            def weights_of(e):
                if e >= 1:
                    pe.wait_ge(wb_ready, e)
                pe.matmul(bank[4][:, 0:NT], sel[:, e, :], wT[:, :], start=True, stop=True).then_inc(wb_ps, 1)

            up_w1(2)
            up_w3(2)
            up_w1(3)
            pe.wait_ge(wparts_ready, 1)
            for b in range(NB):
                last = pe.transpose(bank[4][0:2 * E, b * TB:(b + 1) * TB],
                                    wparts[:, b, :, :].rearrange("p a e -> p (a e)").bitcast(F32),
                                    ident[0:TB, 0:TB])
            last.then_inc(wT_ps, 1)
            up_w3(3)
            pe.wait_ge(wT_ready, 1)
            pe.wait_ge(sel_ready, 1)
            weights_of(0)
            for i in range(4, NCH + LAG):
                if i < NCH:
                    up_w1(i)
                    up_w3(i)
                    if weights_beside(i):
                        weights_of(weights_beside(i))
                if i >= LAG:
                    down(i - LAG)
            for n in range(2):
                pe.wait_ge(yT_ready, n + 1)
                for i in range(2):
                    b = 2 * n + i
                    last = pe.transpose(bank[4 + n][0:TB, i * C:(i + 1) * C], yT[:, b * TB:(b + 1) * TB], ident)
                last.then_inc(y_ps, 1)


def kernel(x, ctx_1024, mask_BxS2xS_ik0, L0_attn_W1q, L0_attn_b1q, L0_attn_W2q, L0_attn_b2q, L0_attn_W1k,
           L0_attn_b1k, L0_attn_W2k, L0_attn_b2k, L0_attn_W1v, L0_attn_b1v, L0_attn_W2v, L0_attn_b2v,
           L0_attn_ln_w, L0_attn_ln_b, L0_xattn_ln_w, L0_xattn_ln_b, L0_xattn_Wq, L0_xattn_Wkv,
           L0_xattn_Wout, L0_ffn_gate_w, L0_ffn_w1, L0_ffn_w3, L0_ffn_w2):
    import concourse.bacc as bacc
    from concourse.bass_utils import run_bass_kernel_spmd

    a = np.asarray
    INNER = H * DH

    def by_heads(w):
        return a(w).reshape(H // 2, 2 * DH, C).transpose(1, 0, 2)

    wkv = a(L0_xattn_Wkv)
    consts = np.zeros((128, 128 + TB + GT + NB + E), np.float32)
    consts[:, 0:128] = np.eye(128)
    j, i = np.arange(TB)[:, None], np.arange(TB)[None, :]
    consts[0:TB, 128:128 + TB] = ((j <= i) & (j // SEQ == i // SEQ)) / np.float32(SCORE_SCALE)
    consts[:, 128 + TB:128 + TB + GT] = np.arange(128)[:, None] % GT == np.arange(GT)[None, :]
    batch = (np.arange(NB)[None, :] * TB + np.arange(TB)[:, None]) // SEQ
    consts[0:TB, 128 + TB + GT:128 + TB + GT + NB] = NV * (batch + 1)
    consts[:, 128 + TB + GT + NB:] = np.arange(E)

    arrays = {
        "x": a(x).reshape(NT, C),
        "ctx_rows": a(ctx_1024).reshape(BATCH * NV, C),
        "mask": a(mask_BxS2xS_ik0).transpose(0, 2, 1).reshape(NB, TB, NV),
        "w_attn": np.stack([a(w) for w in (L0_attn_W1q, L0_attn_W1k, L0_attn_W1v,
                                           L0_attn_W2q, L0_attn_W2k, L0_attn_W2v)], axis=1),
        "cols": np.stack([a(b) for b in (L0_attn_b1q, L0_attn_b1k, L0_attn_b1v, L0_attn_b2q, L0_attn_b2k,
                                         L0_xattn_ln_w, L0_xattn_ln_b)], axis=1),
        "rows": np.stack([a(L0_attn_b2v), a(L0_attn_ln_w), a(L0_attn_ln_b)]),
        "w_x": np.stack([by_heads(a(L0_xattn_Wq).T), by_heads(wkv[:, 0:INNER].T),
                         by_heads(wkv[:, INNER:].T), by_heads(L0_xattn_Wout)], axis=1),
        "w_gate": a(L0_ffn_gate_w),
        "w_ffn": np.stack([a(L0_ffn_w1), a(L0_ffn_w3),
                           a(L0_ffn_w2).reshape(E, FC, 128, C).transpose(0, 2, 1, 3).reshape(E, 128, F)],
                          axis=2),
        "consts": consts,
    }
    arrays = {name: np.ascontiguousarray(v) for name, v in arrays.items()}
    nc = bacc.Bacc("TRN2", target_bir_lowering=False, num_devices=1)
    args = [nc.dram_tensor(name, v.shape, mybir.dt.from_np(v.dtype), kind="ExternalInput").ap()
            for name, v in arrays.items()]
    out = nc.dram_tensor("out", (NT, C), F32, kind="ExternalOutput").ap()
    decoder_layer(nc, *args, out)
    r = run_bass_kernel_spmd(nc, [arrays], core_ids=[0])
    return r.results[0]["out"].reshape(BATCH, SEQ, C)
```
